# Optimizing a Trainium2 kernel written in Bass

```python
import numpy as np
import jax
import jax.numpy as jnp

def _softmax(x, axis=-1):
    return jax.nn.softmax(x, axis=axis)

def _gelu(x):
    return jax.nn.gelu(x, approximate=True)

def _silu(x):
    return jax.nn.silu(x)

def _sigmoid(x):
    return jax.nn.sigmoid(x)

def _layernorm(x, axis=-1, eps=1e-05):
    m = jnp.mean(x, axis=axis, keepdims=True)
    v = jnp.var(x, axis=axis, keepdims=True)
    return (x - m) / jnp.sqrt(v + eps)

def _scatter_add(tgt, idx, src, axis=0):
    return tgt.at[idx].add(src)

def _segment_sum(src, seg, n):
    return jax.ops.segment_sum(src, seg, n)
kernel_name = 'mk_adj_ffn_d1_adj_r2_527156'

def setup_inputs(seed: int=0):
    np.random.seed(seed)
    _w = jnp.asarray

    def _rec_inputs():
        import jax
        import jax.numpy as jnp
        _gk = jax.random.key(seed)
        x = -0.0005207 + 1.001 * jax.random.normal(jax.random.fold_in(_gk, 1), (2048, 256), jnp.float32)
        _a = jax.random.bernoulli(jax.random.fold_in(_gk, 2), 0.00390625, (2048, 2048))
        _af = _a.astype(jnp.float32)
        adj = _af
        return (x, adj)
    x, adj = _rec_inputs()

    def _L0_gnn_setup():
        import jax, jax.numpy as jnp
        import numpy as np
        N = 2048
        INPUT_DIM = 256
        KEY_DIM = 64
        OUT_DIM = 256
        N_HEADS = 8

        def _xavier_normal(key, shape, gain):
            fan_in, fan_out = (shape[-2], shape[-1])
            std = gain * (2.0 / (fan_in + fan_out)) ** 0.5
            return jax.random.normal(key, shape, dtype=jnp.float32) * std
        key = jax.random.key(seed)
        kx, ka, kk, kq, kv, ko = jax.random.split(key, 6)
        gain = 2.0 ** 0.5
        node_matrix = jax.random.normal(kx, (N, INPUT_DIM), dtype=jnp.float32)
        adjacency_matrix = jax.random.randint(ka, (N, N), 0, 2).astype(jnp.float32)
        Wks = _xavier_normal(kk, (N_HEADS, INPUT_DIM, KEY_DIM), gain)
        Wqs = _xavier_normal(kq, (N_HEADS, INPUT_DIM, KEY_DIM), gain)
        Wvs = _xavier_normal(kv, (N_HEADS, INPUT_DIM, KEY_DIM), gain)
        Wo = _xavier_normal(ko, (N_HEADS, KEY_DIM, OUT_DIM), gain)
        return {'node_matrix': node_matrix, 'adjacency_matrix': adjacency_matrix, 'Wks': Wks, 'Wqs': Wqs, 'Wvs': Wvs, 'Wo': Wo}
    _L0_gnn_all = _L0_gnn_setup()
    _L0_gnn_in = {k: v for k, v in _L0_gnn_all.items() if k in ('Wks', 'Wqs', 'Wvs', 'Wo')}
    del _L0_gnn_all

    def _L0_ffn_setup():
        import jax, jax.numpy as jnp
        import numpy as np
        B, S, D = (4, 1024, 256)
        I = 192
        E = 16
        K = 2

        def _inv_softplus(v):
            return float(np.log(np.expm1(v)))

        def swiglu5(h, alpha, gate_scale, up_shift, gate_clamp_raw, up_clamp_raw):
            gate_clamp = jax.nn.softplus(gate_clamp_raw)
            up_clamp = jax.nn.softplus(up_clamp_raw)
            g = jnp.clip(h[..., ::2], -gate_clamp, gate_clamp)
            u = jnp.clip(h[..., 1::2], -up_clamp, up_clamp)
            return g * jax.nn.sigmoid(g * alpha) * gate_scale * (u + up_shift)
        key = jax.random.key(seed)
        ks = jax.random.split(key, 10)
        std = 0.02
        raw = _inv_softplus(7.0)
        act = jnp.array([1.702, 1.0, 1.0, raw, raw], dtype=jnp.float32)
        return {'x': jax.random.normal(ks[0], (B, S, D), dtype=jnp.float32), 'gate_w': jax.random.normal(ks[1], (D, E), dtype=jnp.float32) * 0.01, 'gate_b': jnp.zeros((E,), dtype=jnp.float32), 'shared_w1': jax.random.normal(ks[2], (D, 2 * I), dtype=jnp.float32) * std, 'shared_b1': jnp.zeros((2 * I,), dtype=jnp.float32), 'shared_w2': jax.random.normal(ks[3], (I, D), dtype=jnp.float32) * std, 'shared_b2': jnp.zeros((D,), dtype=jnp.float32), 'shared_act': act, 'expert_w1': jax.random.normal(ks[4], (E, D, 2 * I), dtype=jnp.float32) * std, 'expert_b1': jnp.zeros((E, 2 * I), dtype=jnp.float32), 'expert_w2': jax.random.normal(ks[5], (E, I, D), dtype=jnp.float32) * std, 'expert_b2': jnp.zeros((E, D), dtype=jnp.float32), 'expert_act': jnp.tile(act[None, :], (E, 1))}
    _L0_ffn_all = _L0_ffn_setup()
    _L0_ffn_in = {k: v for k, v in _L0_ffn_all.items() if k in ('gate_w', 'gate_b', 'shared_w1', 'shared_b1', 'shared_w2', 'shared_b2', 'shared_act', 'expert_w1', 'expert_b1', 'expert_w2', 'expert_b2', 'expert_act')}
    del _L0_ffn_all
    return {'x': x, 'adj': adj, 'L0_gnn_Wks': _L0_gnn_in['Wks'], 'L0_gnn_Wqs': _L0_gnn_in['Wqs'], 'L0_gnn_Wvs': _L0_gnn_in['Wvs'], 'L0_gnn_Wo': _L0_gnn_in['Wo'], 'L0_ffn_gate_w': _L0_ffn_in['gate_w'], 'L0_ffn_gate_b': _L0_ffn_in['gate_b'], 'L0_ffn_shared_w1': _L0_ffn_in['shared_w1'], 'L0_ffn_shared_b1': _L0_ffn_in['shared_b1'], 'L0_ffn_shared_w2': _L0_ffn_in['shared_w2'], 'L0_ffn_shared_b2': _L0_ffn_in['shared_b2'], 'L0_ffn_shared_act': _L0_ffn_in['shared_act'], 'L0_ffn_expert_w1': _L0_ffn_in['expert_w1'], 'L0_ffn_expert_b1': _L0_ffn_in['expert_b1'], 'L0_ffn_expert_w2': _L0_ffn_in['expert_w2'], 'L0_ffn_expert_b2': _L0_ffn_in['expert_b2'], 'L0_ffn_expert_act': _L0_ffn_in['expert_act']}

def reference(x, adj, L0_gnn_Wks, L0_gnn_Wqs, L0_gnn_Wvs, L0_gnn_Wo, L0_ffn_gate_w, L0_ffn_gate_b, L0_ffn_shared_w1, L0_ffn_shared_b1, L0_ffn_shared_w2, L0_ffn_shared_b2, L0_ffn_shared_act, L0_ffn_expert_w1, L0_ffn_expert_b1, L0_ffn_expert_w2, L0_ffn_expert_b2, L0_ffn_expert_act):
    import jax
    import jax.numpy as jnp

    def _L0_gnn_ref(node_matrix, adjacency_matrix, Wks, Wqs, Wvs, Wo):
        import jax, jax.numpy as jnp
        import numpy as np
        N = 2048
        INPUT_DIM = 256
        KEY_DIM = 64
        OUT_DIM = 256
        N_HEADS = 8

        def _xavier_normal(key, shape, gain):
            fan_in, fan_out = (shape[-2], shape[-1])
            std = gain * (2.0 / (fan_in + fan_out)) ** 0.5
            return jax.random.normal(key, shape, dtype=jnp.float32) * std
        n = adjacency_matrix.shape[0]
        adj = jnp.maximum(adjacency_matrix, jnp.eye(n, dtype=adjacency_matrix.dtype))
        keys = jnp.einsum('nj,hjk->hnk', node_matrix, Wks)
        queries = jnp.einsum('nj,hjk->hnk', node_matrix, Wqs)
        values = jnp.einsum('nj,hjk->hnk', node_matrix, Wvs)
        key_dim = Wks.shape[-1]
        atts = jnp.einsum('hqk,hmk->hqm', queries, keys) / key_dim ** 0.5
        atts = atts - 1e+16 * (1.0 - adj)[None, :, :]
        atts = jax.nn.softmax(atts, axis=-1)
        return jnp.einsum('hqm,hmk,hko->qo', atts, values, Wo)

    def _L0_ffn_ref(x, gate_w, gate_b, shared_w1, shared_b1, shared_w2, shared_b2, shared_act, expert_w1, expert_b1, expert_w2, expert_b2, expert_act):
        import jax, jax.numpy as jnp
        import numpy as np
        B, S, D = (4, 1024, 256)
        I = 192
        E = 16
        K = 2

        def _inv_softplus(v):
            return float(np.log(np.expm1(v)))

        def swiglu5(h, alpha, gate_scale, up_shift, gate_clamp_raw, up_clamp_raw):
            gate_clamp = jax.nn.softplus(gate_clamp_raw)
            up_clamp = jax.nn.softplus(up_clamp_raw)
            g = jnp.clip(h[..., ::2], -gate_clamp, gate_clamp)
            u = jnp.clip(h[..., 1::2], -up_clamp, up_clamp)
            return g * jax.nn.sigmoid(g * alpha) * gate_scale * (u + up_shift)
        shape = x.shape
        xf = x.reshape(-1, shape[-1])
        h = xf @ shared_w1 + shared_b1
        t = swiglu5(h, shared_act[0], shared_act[1], shared_act[2], shared_act[3], shared_act[4])
        z = t @ shared_w2 + shared_b2
        gate_logits = xf @ gate_w + gate_b
        gate_probs = jax.nn.softmax(gate_logits, -1)
        w, idx = jax.lax.top_k(gate_probs, K)
        w = w / jnp.sum(w, axis=-1, keepdims=True)
        cw = jnp.sum(jax.nn.one_hot(idx, E, dtype=xf.dtype) * w[..., None], axis=1)
        he = jnp.einsum('nd,edh->enh', xf, expert_w1) + expert_b1[:, None, :]
        a = expert_act
        te = swiglu5(he, a[:, 0, None, None], a[:, 1, None, None], a[:, 2, None, None], a[:, 3, None, None], a[:, 4, None, None])
        oe = jnp.einsum('enh,ehd->end', te, expert_w2) + expert_b2[:, None, :]
        y = jnp.einsum('ne,end->nd', cw, oe)
        return (y + z).reshape(shape)
    x = x + _L0_gnn_ref(_layernorm(x, axis=-1), adj, L0_gnn_Wks, L0_gnn_Wqs, L0_gnn_Wvs, L0_gnn_Wo)
    x = x + _L0_ffn_ref(_layernorm(x, axis=-1)[None], L0_ffn_gate_w, L0_ffn_gate_b, L0_ffn_shared_w1, L0_ffn_shared_b1, L0_ffn_shared_w2, L0_ffn_shared_b2, L0_ffn_shared_act, L0_ffn_expert_w1, L0_ffn_expert_b1, L0_ffn_expert_w2, L0_ffn_expert_b2, L0_ffn_expert_act)[0]
    return x

_drawn_inputs = setup_inputs


def setup_inputs(seed=0):
    import zlib

    import numpy as np

    out = dict(_drawn_inputs(seed))
    spreads = {'L0_ffn_gate_b': (0.0, 0.407),
     'L0_ffn_shared_b1': (0.0, 0.8),
     'L0_ffn_shared_b2': (0.0, 0.296),
     'L0_ffn_expert_b1': (0.0, 0.8),
     'L0_ffn_expert_b2': (0.0, 0.413)}
    factors = {'L0_ffn_gate_w': 3.002,
     'L0_ffn_shared_w1': 4.206,
     'L0_ffn_shared_w2': 3.987,
     'L0_ffn_expert_w1': 5.772,
     'L0_ffn_expert_w2': 5.371}
    for name, (base, spread) in spreads.items():
        noise = np.random.default_rng([zlib.crc32(name.encode()), seed]).standard_normal(out[name].shape)
        drawn = base * np.exp(spread * noise) if base else spread * noise
        out[name] = jnp.asarray(drawn.astype(out[name].dtype))
    for name, factor in factors.items():
        out[name] = (out[name] * factor).astype(out[name].dtype)
    return out
```

```python
from contextlib import ExitStack

import concourse.bass as bass
from concourse import mybir

ALU = mybir.AluOpType
ACT = mybir.ActivationFunctionType
F32 = mybir.dt.float32
F32R = mybir.dt.float32r
I8 = mybir.dt.int8
U32 = mybir.dt.uint32
I32 = mybir.dt.int32
AX_X = mybir.AxisListType.X

P = 128
MASK_EXP = 53
LN_EPS = 1e-5


def f32(ap):
    return ap.bitcast(F32)


def attention_block(nc, sem, xacc, ident, x, adj, Wks, Wqs, Wvs, Wo):
    N, D = x.shape
    H, _, DK = Wks.shape
    NT = N // P
    J = D // P
    CQ = 512
    TC = CQ // P
    NC = N // CQ
    SLOT = 1024
    Q_SCALE = 2.0 ** -MASK_EXP * DK ** -0.5
    EXP_SCALE = 2.0 ** MASK_EXP

    with ExitStack() as ctx:
        def sb(name, shape, dt=F32):
            return ctx.enter_context(nc.sbuf_tensor(name, shape, dt))

        def psum(name, shape, dt=F32):
            return ctx.enter_context(nc.psum_tensor(name, shape, dt))

        mask = sb("mask", [P, NT, N], I8)
        xhT = sb("xhT", [P, J, N], F32R)
        xlT = sb("xlT", [P, J, N], F32R)
        kh = sb("kh", [P, N], F32R)
        kl = sb("kl", [P, N], F32R)
        q = sb("q", [P, 2, CQ], F32R)
        v = sb("v", [P, NT, 2 * DK], F32R)
        pr = sb("pr", [P, 2 * TC, N])
        ph = sb("ph", [P, 2, CQ], F32R)
        pl = sb("pl", [P, 2, CQ], F32R)
        oh = sb("oh", [P, CQ], F32R)
        ol = sb("ol", [P, CQ], F32R)
        raw_qkv = sb("raw_qkv", [P, J, 5, DK])
        wh = sb("wh", [P, J, 5, DK], F32R)
        wl = sb("wl", [P, J, 5, DK], F32R)
        raw_o = sb("raw_o", [P, D])
        woh = sb("woh", [P, D], F32R)
        wol = sb("wol", [P, D], F32R)
        adj_in = sb("adj_in", [P, 2, N // 2])
        stats = sb("stats", [P, NT, 6])
        mv = sb("mv", [P, NT, 2])
        sd = sb("sd", [P, NT])
        rstd = sb("rstd", [P, NT])
        epsc = sb("epsc", [P, 1])
        mx = sb("mx", [P, 2 * TC, 2])
        nbias = sb("nbias", [P, 2 * TC])
        rsum = sb("rsum", [P, 3, TC])
        rinv = sb("rinv", [P, 3, TC])

        slots = [psum(f"slot{i}", [P, SLOT]) for i in range(2)]
        pts = [psum(f"pt{i}", [P, CQ]) for i in range(2)]
        pos = [psum(f"po{i}", [P, CQ]) for i in range(2)]

        s_x = [sem(f"s_x{g}") for g in range(N // CQ)]
        s_adj = [sem("s_adj0"), sem("s_adj1")]
        s_mask = sem("s_mask")
        s_ident = sem("s_ident")
        s_stat = sem("s_stat")
        s_sd = sem("s_sd")
        s_xn = sem("s_xn")
        s_lnt = sem("s_lnt")
        s_lnh = sem("s_lnh")
        s_lnl = sem("s_lnl")
        s_rawqkv = sem("s_rawqkv")
        s_rawo = sem("s_rawo")
        s_wqkv = sem("s_wqkv")
        s_wo = sem("s_wo")
        s_wqkv_used = sem("s_wqkv_used")
        s_wo_used = sem("s_wo_used")
        s_slot = sem("s_slot")
        s_hi = sem("s_hi")
        s_free = sem("s_free")
        s_max = sem("s_max")
        s_prob = sem("s_prob")
        s_pt = sem("s_pt")
        s_ph = sem("s_ph")
        s_pl = sem("s_pl")
        s_pv = sem("s_pv")
        s_oh = sem("s_oh")
        s_ol = sem("s_ol")
        s_rinv = sem("s_rinv")
        s_tick = sem("s_tick")
        s_diag = sem("s_diag")
        s_pool_tick = sem("s_pool_tick")

        def items(c, with_t=True, with_w=True):
            s = [("S", t) for t in range(TC)]
            g = [("T", t) for t in range(TC)] if with_t else []
            w = [("W", 0)] if with_w else []
            if c == 0:
                if not with_t:
                    return [("Q", 0), ("K", 0), ("K", 1), s[0], s[1], ("Q", 1), s[2], s[3], ("V", 0)]
                return [("Q", 0), ("K", 0), g[0], ("K", 1), *w, g[1], s[0], s[1], g[2], ("Q", 1),
                        s[2], g[3], s[3], ("O", 0), ("V", 0)]
            out_ = []
            for t in range(TC):
                out_.append(s[t])
                out_ += g[t:t + 1]
                if t == 0:
                    out_ += w
                if t == 1 and c < NC - 1:
                    out_.append(("Q", c + 1))
            return out_ + [("O", 0)]

        LAST = NC * H
        SLOTS = {"Q": 1, "K": 1, "V": 2, "S": 2, "W": 1}
        HIS = {"Q": 1, "K": 1, "V": 2}

        def plan(n):
            if n >= LAST:
                last_t = [("T", t) for t in range(TC)]
                return [("W", 0)] if n > LAST else last_t[:1] + [("W", 0)] + last_t[1:] + [("O", 0)]
            return items(n % NC, n >= 1, n >= 2)

        def counts(plans):
            return dict(slot=sum(SLOTS.get(k, 0) for p_ in plans for k, _ in p_),
                        hi=sum(HIS.get(k, 0) for p_ in plans for k, _ in p_),
                        kt=sum(NT // TC for p_ in plans for k, _ in p_ if k == "T"),
                        tile=sum(1 for p_ in plans for k, _ in p_ if k == "S"),
                        chunk=sum(1 for p_ in plans for k, _ in p_ if k == "O"),
                        w=sum(1 for p_ in plans for k, _ in p_ if k == "W"))

        PRO = 2
        BODY = NC
        LOOPS = H - 1
        START = counts([plan(n) for n in range(PRO)])
        PER = counts([plan(n) for n in range(PRO, PRO + BODY)])

        class Count:

            def __init__(self, base, fixed):
                self.base, self.fixed, self.done = base, fixed, dict.fromkeys(fixed, 0)

            def at(self, key, more=0):
                k = self.done[key] + more
                return k + self.base[key]

            def parity(self, key, more=0):
                return (self.fixed[key] + self.done[key] + more) % 2

        def attention(eng, step, keys):
            c = Count(dict.fromkeys(START, 0), dict.fromkeys(START, 0))
            for n in range(PRO):
                step(c, n, 0)
            with eng.Fori(0, LOOPS) as i:
                base = {k: eng.snap(i * PER[k] + START[k]) for k in keys}
                head = eng.snap(i)
                c = Count(base, START)
                for n in range(PRO, PRO + BODY):
                    step(c, n, head + n // NC)
            total = {k: START[k] + LOOPS * PER[k] for k in START}
            c = Count(total, total)
            for n in range(PRO + LOOPS * BODY, LAST + 2):
                step(c, n, n // NC)

        block = ctx.enter_context(nc.Block())

        def load_head(eng, h):
            for s_, w in ((0, Wqs), (1, Wqs), (2, Wks), (3, Wks), (4, Wvs)):
                src = w[bass.ds(h, 1), :, :].rearrange("a (j p) k -> p (a j) k", p=P)
                eng.dma_start(raw_qkv[:, :, s_, :], src).then_inc(s_rawqkv, 16)

        def load_wo(eng, h):
            for half in range(2):
                eng.dma_start(raw_o[half * DK:(half + 1) * DK, :],
                              Wo[bass.ds(h, 1), :, :].rearrange("a k d -> (a k) d")).then_inc(s_rawo, 16)

        @block.sync
        def _(sp):
            for g in range(NT // TC):
                sp.dma_start(xacc[:, g * TC:(g + 1) * TC, :],
                             x[g * TC * P:(g + 1) * TC * P, :].rearrange("(t p) d -> p t d", p=P)).then_inc(s_x[g], 16)
            load_head(sp, 0)
            load_wo(sp, 0)
            for t in range(2 * NT):
                if t >= 2:
                    sp.wait_ge(s_mask, t - 1)
                sp.dma_start(adj_in[:, t % 2, :],
                             adj[t // 2 * P:(t // 2 + 1) * P, t % 2 * (N // 2):(t % 2 + 1) * (N // 2)]).then_inc(s_adj[t % 2], 16)
            with sp.Fori(1, H) as h:
                sp.wait_ge(s_wqkv, h * 2)
                load_head(sp, h)
                sp.wait_ge(s_wo, h * 2)
                load_wo(sp, h)

        @block.gpsimd
        def _(pool):
            pool.memset(ident[:, :], 0.0).then_inc(s_ident, 1)
            pool.wait_ge(s_ident, 1)
            pool.affine_select(out=ident[:, :], in_=ident[:, :], compare_op=ALU.not_equal, fill=1.0, base=0,
                               pattern=[[-1, P]], channel_multiplier=1).then_inc(s_ident, 1)

            def split_qkv(h):
                pool.wait_ge(s_rawqkv, (h + 1) * 80)
                pool.sem_inc(s_pool_tick)
                pool.tensor_copy(wh[:, :, :, :], raw_qkv[:, :, :, :]).then_inc(s_wqkv, 1)
                pool.wait_ge(s_wqkv, h * 2 + 1)
                pool.tensor_tensor(wl[:, :, :, :], raw_qkv[:, :, :, :], f32(wh[:, :, :, :]), ALU.subtract).then_inc(s_wqkv, 1)

            def split_wo(h):
                pool.wait_ge(s_rawo, (h + 1) * 32)
                pool.sem_inc(s_pool_tick)
                pool.tensor_copy(woh[:, :], raw_o[:, :]).then_inc(s_wo, 1)
                pool.wait_ge(s_wo, h * 2 + 1)
                pool.tensor_tensor(wol[:, :], raw_o[:, :], f32(woh[:, :]), ALU.subtract).then_inc(s_wo, 1)

            split_qkv(0)
            split_wo(0)
            pool.wait_ge(s_ident, 2)
            for t in range(2 * NT):
                qt, half = t // 2, t % 2
                pool.wait_ge(s_adj[half], 16 * (qt + 1))
                src = adj_in[:, half, :]
                col = qt * P - half * (N // 2)
                if 0 <= col < N // 2:
                    d = src[:, col:col + P]
                    pool.affine_select(out=d, in_=d, compare_op=ALU.not_equal, fill=1.0, base=0,
                                       pattern=[[-1, P]], channel_multiplier=1).then_inc(s_diag, 1)
                    pool.wait_ge(s_diag, qt + 1)
                pool.tensor_scalar(mask[:, qt, half * (N // 2):(half + 1) * (N // 2)], src, -1.0, None,
                                   ALU.add).then_inc(s_mask, 1)
            with pool.Fori(1, H) as h:
                pool.wait_ge(s_wqkv_used, h)
                split_qkv(h)
                pool.wait_ge(s_wo_used, h)
                split_wo(h)

        def wait_weights(eng, s, h):
            eng.wait_ge(s, h * 2 + 2)

        @block.tensor
        def _(pe):
            pe.wait_ge(s_ident, 2)
            for g in range(NT // TC):
                if g >= 2:
                    pe.wait_ge(s_lnl, g - 1)
                for t in range(TC):
                    pe.wait_ge(s_xn, g * TC + t + 1)
                    for j in range(J):
                        last = pe.transpose(slots[g % 2][:, j * CQ + t * P:j * CQ + (t + 1) * P],
                                            pr[:, g % 2 * TC + t, j * P:(j + 1) * P], ident[:, :])
                last.then_inc(s_lnt, 1)
            pe.wait_ge(s_lnl, NT // TC)

            def triple(o, lh, ll, rh, rl, first, last):
                pe.matmul(o, lh, rh, start=first, stop=False)
                pe.matmul(o, ll, rh, start=False, stop=False)
                return pe.matmul(o, lh, rl, start=False, stop=last)

            def slot(c):
                if c.fixed["slot"] + c.done["slot"] >= 2:
                    pe.wait_ge(s_free, c.at("slot", -1))
                c.done["slot"] += 1
                return slots[c.parity("slot", -1)]

            def step(c, n, head):
                ch = n % NC
                for kind, a in plan(n):
                    if kind == "Q":
                        o = slot(c)
                        if a == 0:
                            wait_weights(pe, s_wqkv, head)
                        for j in range(J):
                            last = triple(o[:, 0:CQ], wh[:, j, 0:2, :], wl[:, j, 0:2, :],
                                          xhT[:, j, a * CQ:(a + 1) * CQ], xlT[:, j, a * CQ:(a + 1) * CQ], j == 0, j == J - 1)
                        last.then_inc(s_slot, 1)
                        if a == NC - 1:
                            pe.wait_ge(s_slot, c.at("slot"))
                            pe.sem_inc(s_wqkv_used)
                    elif kind == "K":
                        o = slot(c)
                        for b in range(2):
                            for j in range(J):
                                cols = slice((2 * a + b) * CQ, (2 * a + b + 1) * CQ)
                                last = triple(o[:, b * CQ:(b + 1) * CQ], wh[:, j, 2:4, :], wl[:, j, 2:4, :],
                                              xhT[:, j, cols], xlT[:, j, cols], j == 0, j == J - 1)
                        last.then_inc(s_slot, 1)
                    elif kind == "V":
                        for half in range(2):
                            o = slot(c)
                            for t in range(NT // 2):
                                tt = half * (NT // 2) + t
                                for j in range(J):
                                    last = triple(o[:, t * DK:(t + 1) * DK], xhT[:, j, tt * P:(tt + 1) * P],
                                                  xlT[:, j, tt * P:(tt + 1) * P], wh[:, j, 4, :], wl[:, j, 4, :],
                                                  j == 0, j == J - 1)
                            last.then_inc(s_slot, 1)
                    elif kind == "S":
                        for half in range(2):
                            o = slot(c)
                            if half == 0:
                                need = {0: {0: 1}}.get(n, {}).get(a)
                                pe.wait_ge(s_free, c.at("slot", -1) if a == 0 or (ch == 0) else c.at("slot", -2))
                            for b in range(2):
                                cols = slice((2 * half + b) * CQ, (2 * half + b + 1) * CQ)
                                qt = q[:, ch % 2, a * P:(a + 1) * P]
                                pe.matmul(o[:, b * CQ:(b + 1) * CQ], qt, kh[:, cols], start=True, stop=False)
                                last = pe.matmul(o[:, b * CQ:(b + 1) * CQ], qt, kl[:, cols], start=False, stop=True)
                            last.then_inc(s_slot, 1)
                    elif kind == "T":
                        par = (n - 1) % 2
                        per = NT // TC

                        def pv(kt, back):
                            pe.wait_ge(s_pl, c.at("kt", 1 - back))
                            pk = c.parity("kt", -back)
                            pe.matmul(pos[par][:, :], v[:, kt, :], ph[:, pk, :], start=(kt == 0), stop=False)
                            m = pe.matmul(pos[par][:, :], v[:, kt, :], pl[:, pk, :], start=False, stop=(kt == NT - 1))
                            if kt == NT - 1:
                                m.then_inc(s_pv, 1)

                        if a == 0:
                            if n >= 1:
                                extra = sum(1 for k_, _ in plan(n)[:plan(n).index(("T", 0))] if k_ == "S")
                                pe.wait_ge(s_prob, c.at("tile", -extra))
                        for kk in range(per):
                            kt = a * per + kk
                            if c.fixed["kt"] + c.done["kt"] >= 2:
                                pe.wait_ge(s_pl, c.at("kt", -1))
                            for t in range(TC):
                                last = pe.transpose(pts[c.parity("kt")][:, t * P:(t + 1) * P],
                                                    pr[:, par * TC + t, kt * P:(kt + 1) * P], ident[:, :])
                            last.then_inc(s_pt, 1)
                            if kk > 0:
                                pv(kt - 1, 1)
                            c.done["kt"] += 1
                        pv(kt, 1)
                    elif kind == "O":
                        c.done["chunk"] += 1
                    elif kind == "W":
                        o = slot(c)
                        wch = (n - 2) % NC
                        pe.wait_ge(s_ol, c.at("w", 1))
                        if wch == 0:
                            wait_weights(pe, s_wo, head if n >= 2 and (n - 2) // NC == n // NC else head - 1)
                        for t in range(TC):
                            cols = slice(t * P, (t + 1) * P)
                            last = triple(o[:, t * D:(t + 1) * D], oh[:, cols], ol[:, cols], woh[:, :], wol[:, :], True, True)
                        last.then_inc(s_slot, 1)
                        c.done["w"] += 1
                        if wch == NC - 1:
                            pe.wait_ge(s_slot, c.at("slot"))
                            pe.sem_inc(s_wo_used)
                    if kind == "S":
                        c.done["tile"] += 1

            attention(pe, step, ("slot", "kt", "tile", "w"))

        @block.scalar
        def _(act):
            act.wait_ge(s_stat, 2 * NT + 1)
            act.activation(sd[:, :], mv[:, :, 1], ACT.Sqrt, bias=epsc[:, 0:1]).then_inc(s_sd, 1)
            for g in range(NT // TC):
                act.wait_ge(s_lnt, g + 1)
                act.activation(xhT[:, :, g * CQ:(g + 1) * CQ], slots[g % 2][:, :].rearrange("p (j n) -> p j n", j=J),
                               ACT.Copy).then_inc(s_lnh, 1)

            def step(c, n, head):
                ch = n % NC
                par = n % 2
                pending = []

                def exp_tile(t, tile_count):
                    act.wait_ge(s_max, tile_count)
                    act.activation(pr[:, par * TC + t, :], pr[:, par * TC + t, :], ACT.Exp,
                                   bias=nbias[:, par * TC + t:par * TC + t + 1], scale=EXP_SCALE,
                                   accum_out=rsum[:, n % 2, t:t + 1]).then_inc(s_prob, 1)

                for kind, a in plan(n):
                    if kind in ("Q", "K"):
                        act.wait_ge(s_slot, c.at("slot", 1))
                        o = slots[c.parity("slot")]
                        if kind == "Q":
                            act.activation(q[:, a % 2, :], o[:, 0:CQ], ACT.Copy, scale=Q_SCALE).then_inc(s_hi, 1)
                        else:
                            act.activation(kh[:, a * SLOT:(a + 1) * SLOT], o[:, :], ACT.Copy).then_inc(s_hi, 1)
                        c.done["slot"] += 1
                    elif kind == "V":
                        for half in range(2):
                            act.wait_ge(s_slot, c.at("slot", 1))
                            o = slots[c.parity("slot")]
                            act.activation(v[:, half * (NT // 2):(half + 1) * (NT // 2), 0:DK],
                                           o[:, 0:NT // 2 * DK].rearrange("p (t k) -> p t k", k=DK), ACT.Copy).then_inc(s_hi, 1)
                            c.done["slot"] += 1
                    elif kind == "S":
                        c.done["slot"] += 2
                        c.done["tile"] += 1
                        pending.append((a, c.at("tile")))
                        if not any(k_ == "T" for k_, _ in plan(n)):
                            exp_tile(*pending.pop(0))
                    elif kind == "W":
                        c.done["slot"] += 1
                    elif kind == "T":
                        for kk in range(NT // TC):
                            act.wait_ge(s_pt, c.at("kt", 1))
                            pk = c.parity("kt")
                            act.activation(ph[:, pk, :], pts[pk][:, :], ACT.Copy).then_inc(s_ph, 1)
                            c.done["kt"] += 1
                            if kk == 1 and pending:
                                exp_tile(*pending.pop(0))
                    elif kind == "O":
                        while pending:
                            exp_tile(*pending.pop(0))
                        act.wait_ge(s_pv, c.at("chunk", 1))
                        act.activation(oh[:, :], pos[(n - 1) % 2][:, :], ACT.Copy).then_inc(s_oh, 1)
                        c.done["chunk"] += 1

            attention(act, step, ("slot", "kt", "tile", "chunk"))

        @block.vector
        def _(dve):
            dve.memset(epsc[:, :], LN_EPS).then_inc(s_stat, 1)
            for t in range(NT):
                if t % TC == 0:
                    dve.wait_ge(s_x[t // TC], 16)
                dve.bn_stats(stats[:, t, :], xacc[:, t, :]).then_inc(s_stat, 1)
            for t in range(NT):
                dve.wait_ge(s_stat, t + 2)
                dve.bn_aggr(mv[:, t, :], stats[:, t, :]).then_inc(s_stat, 1)
            dve.wait_ge(s_sd, 1)
            dve.reciprocal(rstd[:, :], sd[:, :]).then_inc(s_stat, 1)
            dve.wait_ge(s_stat, 2 * NT + 2)

            def split_rows(g):
                dve.wait_ge(s_lnh, g + 1)
                dve.tensor_tensor(xlT[:, :, g * CQ:(g + 1) * CQ], slots[g % 2][:, :].rearrange("p (j n) -> p j n", j=J),
                                  f32(xhT[:, :, g * CQ:(g + 1) * CQ]), ALU.subtract).then_inc(s_lnl, 1)

            for g in range(NT // TC):
                for t in range(TC):
                    tt = g * TC + t
                    if g >= 2:
                        dve.wait_ge(s_lnt, g - 1)
                    dve.tensor_scalar(pr[:, g % 2 * TC + t, 0:D], xacc[:, tt, :], mv[:, tt, 0:1], rstd[:, tt:tt + 1],
                                      ALU.subtract, ALU.mult).then_inc(s_xn, 1)
                if g >= 1:
                    split_rows(g - 1)
            split_rows(NT // TC - 1)

            def step(c, n, head):
                par = n % 2

                def wait_slot():
                    dve.wait_ge(s_slot, c.at("slot", 1))
                    return slots[c.parity("slot")]

                for kind, a in plan(n):
                    if kind in ("Q", "K", "V"):
                        for half in range(2 if kind == "V" else 1):
                            dve.wait_ge(s_hi, c.at("hi", 1))
                            o = wait_slot()
                            if kind == "Q":
                                m = dve.scalar_tensor_tensor(q[DK:P, a % 2, :], o[DK:P, 0:CQ], Q_SCALE, f32(q[DK:P, a % 2, :]),
                                                             ALU.mult, ALU.subtract)
                            elif kind == "K":
                                cols = slice(a * SLOT, (a + 1) * SLOT)
                                m = dve.tensor_tensor(kl[:, cols], o[:, :], f32(kh[:, cols]), ALU.subtract)
                            else:
                                ts = slice(half * (NT // 2), (half + 1) * (NT // 2))
                                m = dve.tensor_tensor(v[:, ts, DK:2 * DK], o[:, 0:NT // 2 * DK].rearrange("p (t k) -> p t k", k=DK),
                                                      f32(v[:, ts, 0:DK]), ALU.subtract)
                            m.then_inc(s_free, 1)
                            c.done["slot"] += 1
                            c.done["hi"] += 1
                    elif kind == "S":
                        i = par * TC + a
                        qt = n % NC * TC + a
                        if n < NC:
                            dve.wait_ge(s_mask, 2 * (qt + 1))
                        for half in range(2):
                            o = wait_slot()
                            dve.sem_inc(s_tick)
                            dve.tensor_tensor_reduce(pr[:, i, half * SLOT:(half + 1) * SLOT], o[:, :],
                                                     mask[:, qt, half * SLOT:(half + 1) * SLOT], 1.0, -3.0e38,
                                                     ALU.add, ALU.max, mx[:, i, half:half + 1]).then_inc(s_free, 1)
                            c.done["slot"] += 1
                        dve.wait_ge(s_free, c.at("slot"))
                        dve.tensor_scalar(nbias[:, i:i + 1], mx[:, i, 0:1], mx[:, i, 1:2], -EXP_SCALE,
                                          ALU.max, ALU.mult).then_inc(s_max, 1)
                        c.done["tile"] += 1
                    elif kind == "T":
                        for kk in range(NT // TC):
                            dve.wait_ge(s_ph, c.at("kt", 1))
                            pk = c.parity("kt")
                            dve.tensor_tensor(pl[:, pk, :], pts[pk][:, :], f32(ph[:, pk, :]), ALU.subtract).then_inc(s_pl, 1)
                            c.done["kt"] += 1
                            if a == 0 and kk == 0:
                                dve.reciprocal(rinv[:, (n - 1) % 2, :], rsum[:, (n - 1) % 2, :]).then_inc(s_rinv, 1)
                    elif kind == "O":
                        dve.wait_ge(s_oh, c.at("chunk", 1))
                        dve.tensor_tensor(ol[:, :], pos[(n - 1) % 2][:, :], f32(oh[:, :]), ALU.subtract).then_inc(s_ol, 1)
                        c.done["chunk"] += 1
                    elif kind == "W":
                        o = wait_slot()
                        dve.wait_ge(s_rinv, c.at("w", 1))
                        wn = n - 2
                        for t in range(TC):
                            xt = xacc[:, wn % NC * TC + t, :]
                            m = dve.scalar_tensor_tensor(xt, o[:, t * D:(t + 1) * D], rinv[:, wn % 2, t:t + 1], xt,
                                                         ALU.mult, ALU.add)
                        m.then_inc(s_free, 1)
                        c.done["slot"] += 1
                        c.done["w"] += 1

            attention(dve, step, ("slot", "kt", "tile", "chunk", "hi", "w"))


def expert_block(nc, sem, xacc, ident, gate_w, gate_b, shared_w1, shared_b1, shared_w2, shared_b2, shared_act,
                 expert_w1, expert_b1, expert_w2, expert_b2, expert_act, out):
    D = gate_w.shape[0]
    E = gate_w.shape[1]
    HID = shared_w1.shape[1]
    I = HID // 2
    NT = xacc.shape[1]
    N = NT * P
    J = D // P
    KI = 96
    JI = I // KI
    TOPK = 2
    TILES = (TOPK * N + (P - 1) * E) // P
    TILES += TILES % 2
    ALL = NT + TILES
    JT = N // P
    NACT = 7

    with ExitStack() as ctx:
        def sb(name, shape, dt=F32):
            return ctx.enter_context(nc.sbuf_tensor(name, shape, dt))

        def psum(name, shape, dt=F32):
            return ctx.enter_context(nc.psum_tensor(name, shape, dt))

        xs = nc.dram_tensor("expert_rows", [ALL * P, D], F32, kind="Internal").ap()
        ys = nc.dram_tensor("expert_results", [ALL * P, D], F32, kind="Internal").ap()

        w1 = sb("w1", [P, E + 1, J, HID])
        w2 = sb("w2", [KI, E + 1, JI, D])
        b1 = sb("b1", [1, E + 1, HID])
        b2 = sb("b2", [1, E + 1, D])
        gw = sb("gw", [P, J, E])
        gb = sb("gb", [P, E])
        araw = sb("araw", [P, E + 1, 5])
        acts = sb("acts", [P, E + 1, NACT])
        sp_t = sb("sp_t", [P, 4, E + 1, 2])
        ones = sb("ones", [P, P])
        before = sb("before", [P, P])
        zeros = sb("zeros", [P, D])
        iota_e = sb("iota_e", [P, E])
        iota_t = sb("iota_t", [P, TILES])
        iota_j = sb("iota_j", [P, JT])
        xn = sb("xn2", [P, NT, D])
        stats = sb("stats2", [P, NT, 6])
        mv = sb("mv2", [P, NT, 2])
        sd = sb("sd2", [P, NT])
        rstd = sb("rstd2", [P, NT])
        epsc = sb("epsc2", [P, 1])
        xT = sb("xT", [P, 2, J, P])
        logits = sb("logits", [P, NT, E])
        top = sb("top", [P, NT, 8])
        topi = sb("topi", [P, NT, 8], U32)
        topf = sb("topf", [P, TOPK, NT])
        diff = sb("diff", [P, NT])
        e2 = sb("e2", [P, NT])
        den = sb("den", [P, NT])
        cw = sb("cw", [P, TOPK, NT])
        oh = sb("onehot", [P, TOPK, NT, E])
        oh12 = sb("oh12", [P, NT, E])
        big = sb("big", [P, E * TILES])
        ntile = sb("ntile", [P, 6, E])
        place = sb("place", [P, NT, E])
        slotf = sb("slotf", [P, TOPK, NT])
        slot = sb("slot", [P, TOPK, NT], U32)
        eidf = sb("eidf", [P, ALL])
        eid = sb("eid", [P, ALL], I32)
        xin = sb("xin", [P, 2, D])
        actrow = sb("actrow", [P, 2, NACT])
        gg = sb("gg", [P, 2, I])
        uu = sb("uu", [P, 2, I])
        sg = sb("sg", [P, 2, I])
        te = sb("te", [P, 2, I])
        teT = sb("teT", [KI, 2, JI, P])
        yo = sb("yo", [P, 2, D])
        yg = sb("yg", [P, 2, TOPK + 1, D])
        ya = sb("ya", [P, 2, D])

        ps_t = [psum(f"ps_t{i}", [P, 512]) for i in range(2)]
        ps_h = [psum(f"ps_h{i}", [P, 512]) for i in range(2)]
        ps_u = [psum(f"ps_u{i}", [P, 512]) for i in range(2)]
        ps_y = [psum(f"ps_y{i}", [P, 512]) for i in range(2)]

        s_w = sem("e_weights")
        s_gate = sem("e_gate_weights")
        s_act = sem("e_act_table")
        s_const = sem("e_constants")
        s_ln = sem("e_ln")
        s_lnsd = sem("e_lnsd")
        s_xn = sem("e_xn")
        s_gt = sem("e_gate_transposed")
        s_gx = sem("e_gate_copied")
        s_gl = sem("e_gate_logits")
        s_top = sem("e_top")
        s_exp = sem("e_exp")
        s_oh = sem("e_onehot")
        s_cnt = sem("e_counts")
        s_chain = sem("e_chain")
        s_place = sem("e_place")
        s_eid = sem("e_eid")
        s_sp = sem("e_softplus")
        s_rows = sem("e_rows")
        s_scat = sem("e_scattered")
        s_zero = sem("e_zero")
        s_xin = [sem("e_xin0"), sem("e_xin1")]
        s_xt = sem("e_xt")
        s_xc = sem("e_xc")
        s_h = sem("e_h")
        s_row = sem("e_actrow")
        s_clip = sem("e_clip")
        s_row2 = sem("e_gated")
        s_sig = sem("e_sig")
        s_te = sem("e_te")
        s_tt = sem("e_tt")
        s_tc = sem("e_tc")
        s_y = sem("e_y")
        s_yo = sem("e_yo")
        s_ys = [sem("e_ys0"), sem("e_ys1")]
        s_yg = [sem("e_yg0"), sem("e_yg1")]
        s_sum = sem("e_sum")
        s_res = sem("e_res")
        s_out = [sem("e_out0"), sem("e_out1")]

        block = ctx.enter_context(nc.Block())
        PAIRS = ALL // 2

        @block.sync
        def _(sp):
            sp.dma_start(gw[:, :, :], gate_w.rearrange("(j p) e -> p j e", p=P)).then_inc(s_gate, 16)
            sp.dma_start(gb[:, :], gate_b.rearrange("(a e) -> a e", a=1).broadcast_to([P, E])).then_inc(s_gate, 16)
            sp.dma_start(araw[:, 0:E, :], expert_act.rearrange("(a e) k -> a e k", a=1).broadcast_to([P, E, 5])).then_inc(s_act, 16)
            sp.dma_start(araw[:, E, :], shared_act.rearrange("(a k) -> a k", a=1).broadcast_to([P, 5])).then_inc(s_act, 16)
            sp.wait_ge(s_const, 1)
            for t in range(TILES):
                sp.dma_start(xs[(NT + t) * P:(NT + t + 1) * P, :], zeros[:, :]).then_inc(s_zero, 16)
            sp.dma_start(w1[:, E, :, :], shared_w1.rearrange("(j p) h -> p j h", p=P)).then_inc(s_w, 16)
            sp.dma_start(w2[:, E, :, :], shared_w2.rearrange("(j p) d -> p j d", p=KI)).then_inc(s_w, 16)
            sp.dma_start(b1[:, E, :], shared_b1.rearrange("(a h) -> a h", a=1)).then_inc(s_w, 16)
            sp.dma_start(b2[:, E, :], shared_b2.rearrange("(a h) -> a h", a=1)).then_inc(s_w, 16)
            sp.dma_start(b1[:, 0:E, :], expert_b1.rearrange("(a e) h -> a e h", a=1)).then_inc(s_w, 16)
            sp.dma_start(b2[:, 0:E, :], expert_b2.rearrange("(a e) h -> a e h", a=1)).then_inc(s_w, 16)
            for e in range(E):
                sp.dma_start(w1[:, e, :, :], expert_w1[e].rearrange("(j p) h -> p j h", p=P)).then_inc(s_w, 16)
                sp.dma_start(w2[:, e, :, :], expert_w2[e].rearrange("(j p) d -> p j d", p=KI)).then_inc(s_w, 16)
            sp.wait_ge(s_xn, NT)
            sp.dma_start(xs[0:N, :].rearrange("(t p) d -> p t d", p=P), xn[:, :, :]).then_inc(s_rows, 16)
            sp.wait_ge(s_rows, 16)
            sp.wait_ge(s_scat, 16 * TOPK * NT)

            def load(i, b):
                sp.dma_start(xin[:, b, :], xs[bass.ds(i * P, P), :]).then_inc(s_xin[b], 16)

            for b in range(2):
                load(b, b)
            with sp.Fori(1, PAIRS) as ip:
                for b in range(2):
                    sp.wait_ge(s_xt, ip * 2 + b - 1)
                    load(ip * 2 + b, b)

            for t in range(NT):
                sp.wait_ge(s_res, t + 1)
                sp.dma_start(out[t * P:(t + 1) * P, :], ya[:, t % 2, :]).then_inc(s_out[t % 2], 16)
            for b in range(2):
                sp.wait_ge(s_out[b], 16 * (NT // 2))

        @block.gpsimd
        def _(pool):
            pool.memset(zeros[:, :], 0.0).then_inc(s_const, 1)
            pool.memset(ones[:, :], 1.0).then_inc(s_const, 1)
            pool.memset(before[:, :], 1.0).then_inc(s_const, 1)
            pool.wait_ge(s_const, 3)
            pool.affine_select(out=before[:, :], in_=before[:, :], compare_op=ALU.is_gt, fill=0.0, base=0,
                               pattern=[[1, P]], channel_multiplier=-1).then_inc(s_const, 1)
            pool.iota(iota_e[:, :], [[1, E]], base=0, channel_multiplier=0, allow_small_or_imprecise_dtypes=True).then_inc(s_const, 1)
            pool.iota(iota_t[:, :], [[1, TILES]], base=0, channel_multiplier=0, allow_small_or_imprecise_dtypes=True).then_inc(s_const, 1)
            pool.iota(iota_j[:, :], [[P, JT]], base=0, channel_multiplier=0, allow_small_or_imprecise_dtypes=True).then_inc(s_const, 1)
            pool.wait_ge(s_place, 1)
            pool.wait_ge(s_zero, 16 * TILES)
            for k in range(TOPK):
                for t in range(NT):
                    pool.indirect_dma_start(xs, bass.IndirectOffsetOnAxis(slot[:, k, t:t + 1], 0),
                                            xn[:, t, :], None).then_inc(s_scat, 16)
            pool.wait_ge(s_ys[0], 16 * PAIRS)
            pool.wait_ge(s_ys[1], 16 * PAIRS)
            for t in range(NT):
                b = t % 2
                if t >= 2:
                    pool.wait_ge(s_sum, t - 1)
                pool.dma_start(yg[:, b, TOPK, :], ys[t * P:(t + 1) * P, :]).then_inc(s_yg[b], 16)
                for k in range(TOPK):
                    pool.indirect_dma_start(yg[:, b, k, :], None, ys,
                                            bass.IndirectOffsetOnAxis(slot[:, k, t:t + 1], 0)).then_inc(s_yg[b], 16)

        @block.tensor
        def _(pe):
            pe.wait_ge(s_gate, 32)
            for t in range(NT):
                b = t % 2
                pe.wait_ge(s_xn, t + 1)
                if t >= 2:
                    pe.wait_ge(s_gx, t - 1)
                for j in range(J):
                    last = pe.transpose(ps_t[b][:, j * P:(j + 1) * P], xn[:, t, j * P:(j + 1) * P], ident[:, :])
                last.then_inc(s_gt, 1)
                pe.wait_ge(s_gx, t + 1)
                for j in range(J):
                    last = pe.matmul(ps_h[0][:, t * E:(t + 1) * E], xT[:, b, j, :], gw[:, j, :], start=(j == 0), stop=(j == J - 1))
                last.then_inc(s_gl, 1)
            pe.wait_ge(s_oh, 1)
            pe.wait_ge(s_const, 4)
            pe.matmul(ps_u[0][:, 0:NT * E], before[:, :], oh12[:, :, :], start=True, stop=False)
            for t in range(NT - 1):
                rest = NT - 1 - t
                pe.matmul(ps_u[0][:, (t + 1) * E:NT * E], ones[:, :],
                          oh12[:, t:t + 1, :].broadcast_to([P, rest, E]), start=False, stop=(t == NT - 2))
            for t in range(NT):
                last = pe.matmul(ps_u[1][:, 0:E], ones[:, :], oh12[:, t, :], start=(t == 0), stop=(t == NT - 1))
            last.then_inc(s_cnt, 1)

            pe.wait_ge(s_w, 16 * (6 + 2 * E))
            pe.wait_ge(s_eid, 1)

            def first(i, b, ip):
                e = pe.value_load(eid[0:1, bass.ds(i, 1)], min_val=0, max_val=E)
                pe.wait_ge(s_xin[b], (ip + 1) * 16)
                for j in range(J):
                    last = pe.transpose(ps_t[b][:, j * P:(j + 1) * P], xin[:, b, j * P:(j + 1) * P], ident[:, :])
                last.then_inc(s_xt, 1)
                pe.wait_ge(s_xc, i + 1)
                for j in range(J):
                    pe.matmul(ps_h[b][:, 0:HID], xT[:, b, j, :], w1[:, bass.ds(e, 1), j, :], start=(j == 0), stop=False)
                pe.matmul(ps_h[b][:, 0:HID], ones[0:1, :], b1[0:1, bass.ds(e, 1), :], start=False, stop=True).then_inc(s_h, 1)

            def second(i, b, ip):
                e = pe.value_load(eid[0:1, bass.ds(i, 1)], min_val=0, max_val=E)
                pe.wait_ge(s_te, i + 1)
                for j in range(JI):
                    last = pe.transpose(ps_u[b][0:KI, j * P:(j + 1) * P], te[:, b, j * KI:(j + 1) * KI], ident[:, :])
                last.then_inc(s_tt, 1)
                pe.wait_ge(s_tc, i + 1)
                if not (isinstance(ip, int) and ip == 0):
                    pe.wait_ge(s_yo, i - 1)
                for j in range(JI):
                    pe.matmul(ps_y[b][:, 0:D], teT[:, b, j, :], w2[:, bass.ds(e, 1), j, :], start=(j == 0), stop=False)
                pe.matmul(ps_y[b][:, 0:D], ones[0:1, :], b2[0:1, bass.ds(e, 1), :], start=False, stop=True).then_inc(s_y, 1)

            def pair(ip, last=False):
                i = ip * 2
                first(i + 1, 1, ip)
                second(i, 0, ip)
                if not last:
                    first(i + 2, 0, ip + 1)
                second(i + 1, 1, ip)

            first(0, 0, 0)
            pair(0)
            with pe.Fori(1, PAIRS - 1) as ip:
                pair(ip)
            pair(PAIRS - 1, last=True)

        @block.scalar
        def _(act):
            act.wait_ge(s_ln, 2 * NT + 1)
            act.activation(sd[:, :], mv[:, :, 1], ACT.Sqrt, bias=epsc[:, 0:1]).then_inc(s_lnsd, 1)
            act.wait_ge(s_sp, 3)
            act.activation(sp_t[:, 2, :, :], sp_t[:, 1, :, :], ACT.Exp, scale=-1.0).then_inc(s_sp, 1)
            act.wait_ge(s_sp, 4)
            act.activation(sp_t[:, 3, :, :], sp_t[:, 2, :, :], ACT.Ln, bias=1.0).then_inc(s_sp, 1)
            for t in range(NT):
                act.wait_ge(s_gt, t + 1)
                if t >= 2:
                    act.wait_ge(s_gl, t - 1)
                act.activation(xT[:, t % 2, :, :], ps_t[t % 2][:, 0:J * P], ACT.Copy).then_inc(s_gx, 1)
            act.wait_ge(s_top, 1)
            act.activation(e2[:, :], diff[:, :], ACT.Exp).then_inc(s_exp, 1)
            act.wait_ge(s_gl, NT)

            def copy_x(i, b):
                act.wait_ge(s_xt, i + 1)
                act.activation(xT[:, b, :, :], ps_t[b][:, 0:J * P], ACT.Copy).then_inc(s_xc, 1)

            def finish(i, b, ip):
                act.wait_ge(s_clip, i * 2 + 1)
                act.activation(sg[:, b, :], gg[:, b, :], ACT.Sigmoid, scale=actrow[:, b, 0:1]).then_inc(s_sig, 1)
                act.wait_ge(s_tt, i + 1)
                act.activation(teT[:, b, :, :], ps_u[b][0:KI, 0:JI * P], ACT.Copy).then_inc(s_tc, 1)
                act.wait_ge(s_y, i + 1)
                if not (isinstance(ip, int) and ip == 0):
                    act.wait_ge(s_ys[b], ip * 16)
                act.activation(yo[:, b, :], ps_y[b][:, 0:D], ACT.Copy).then_inc(s_yo, 1)
                act.wait_ge(s_yo, i + 1)
                act.dma_start(ys[bass.ds(i * P, P), :], yo[:, b, :]).then_inc(s_ys[b], 16)

            def pair(ip, last=False):
                i = ip * 2
                copy_x(i + 1, 1)
                finish(i, 0, ip)
                if not last:
                    copy_x(i + 2, 0)
                finish(i + 1, 1, ip)

            copy_x(0, 0)
            pair(0)
            with act.Fori(1, PAIRS - 1) as ip:
                pair(ip)
            pair(PAIRS - 1, last=True)

        @block.vector
        def _(dve):
            chain = [0]

            def link(ins):
                chain[0] += 1
                ins.then_inc(s_chain, 1)
                dve.wait_ge(s_chain, chain[0])

            dve.memset(epsc[:, :], LN_EPS).then_inc(s_ln, 1)
            for t in range(NT):
                dve.bn_stats(stats[:, t, :], xacc[:, t, :]).then_inc(s_ln, 1)
            for t in range(NT):
                dve.wait_ge(s_ln, t + 2)
                dve.bn_aggr(mv[:, t, :], stats[:, t, :]).then_inc(s_ln, 1)
            dve.wait_ge(s_lnsd, 1)
            link(dve.reciprocal(rstd[:, :], sd[:, :]))
            for t in range(NT):
                dve.tensor_scalar(xn[:, t, :], xacc[:, t, :], mv[:, t, 0:1], rstd[:, t:t + 1],
                                  ALU.subtract, ALU.mult).then_inc(s_xn, 1)
            dve.wait_ge(s_act, 32)
            raw = araw[:, :, 3:5]
            dve.tensor_scalar(sp_t[:, 0, :, :], raw, -1.0, None, ALU.mult).then_inc(s_sp, 1)
            dve.wait_ge(s_sp, 1)
            dve.tensor_tensor(sp_t[:, 1, :, :], raw, sp_t[:, 0, :, :], ALU.max).then_inc(s_sp, 1)
            dve.wait_ge(s_sp, 2)
            dve.tensor_scalar(sp_t[:, 0, :, :], raw, 0.0, None, ALU.max).then_inc(s_sp, 1)
            dve.wait_ge(s_sp, 5)
            link(dve.tensor_tensor(acts[:, :, 3:7:2], sp_t[:, 0, :, :], sp_t[:, 3, :, :], ALU.add))
            link(dve.tensor_scalar(acts[:, :, 4:7:2], acts[:, :, 3:7:2], -1.0, None, ALU.mult))
            link(dve.tensor_copy(acts[:, :, 0:3], araw[:, :, 0:3]))
            dve.wait_ge(s_gl, NT)
            link(dve.tensor_tensor(logits[:, :, :], ps_h[0][:, 0:NT * E].rearrange("p (t e) -> p t e", e=E),
                                   gb[:, :].rearrange("p (a e) -> p a e", a=1).broadcast_to([P, NT, E]), ALU.add))
            for t in range(NT):
                dve.max(top[:, t, :], logits[:, t, :]).then_inc(s_chain, 1)
            chain[0] += NT
            dve.wait_ge(s_chain, chain[0])
            for t in range(NT):
                dve.max_index(topi[:, t, :], top[:, t, :], logits[:, t, :]).then_inc(s_chain, 1)
            chain[0] += NT
            dve.wait_ge(s_chain, chain[0])
            dve.tensor_tensor(diff[:, :], top[:, :, 1], top[:, :, 0], ALU.subtract).then_inc(s_top, 1)
            link(dve.tensor_copy(topf[:, :, :].rearrange("p k t -> p t k"), topi[:, :, 0:TOPK]))
            dve.wait_ge(s_const, 7)
            for k in range(TOPK):
                link(dve.tensor_tensor(oh[:, k, :, :], topf[:, k, :].rearrange("p (t a) -> p t a", a=1).broadcast_to([P, NT, E]),
                                       iota_e[:, :].rearrange("p (a e) -> p a e", a=1).broadcast_to([P, NT, E]), ALU.is_equal))
            dve.tensor_tensor(oh12[:, :, :], oh[:, 0, :, :], oh[:, 1, :, :], ALU.add).then_inc(s_oh, 1)
            dve.wait_ge(s_exp, 1)
            link(dve.tensor_scalar(den[:, :], e2[:, :], 1.0, None, ALU.add))
            link(dve.reciprocal(cw[:, 0, :], den[:, :]))
            link(dve.tensor_tensor(cw[:, 1, :], cw[:, 0, :], e2[:, :], ALU.mult))
            dve.wait_ge(s_cnt, 1)
            cnt = ntile[:, 5, :]
            link(dve.tensor_copy(cnt, ps_u[1][:, 0:E]))
            cmp = big[:, 0:E * JT].rearrange("p (e j) -> p e j", j=JT)
            link(dve.tensor_tensor(cmp, cnt.rearrange("p (e a) -> p e a", a=1).broadcast_to([P, E, JT]),
                                   iota_j[:, :].rearrange("p (a j) -> p a j", a=1).broadcast_to([P, E, JT]), ALU.is_gt))
            link(dve.tensor_reduce(ntile[:, 0, :], cmp, AX_X, ALU.add))
            link(dve.tensor_copy(ntile[:, 1, :], ntile[:, 0, :]))
            cur, step = 1, 1
            while step < E:
                link(dve.tensor_copy(ntile[:, 3 - cur, 0:step], ntile[:, cur, 0:step]))
                link(dve.tensor_tensor(ntile[:, 3 - cur, step:E], ntile[:, cur, step:E], ntile[:, cur, 0:E - step], ALU.add))
                cur, step = 3 - cur, 2 * step
            link(dve.tensor_tensor(ntile[:, 3, :], ntile[:, cur, :], ntile[:, 0, :], ALU.subtract))
            link(dve.tensor_scalar(ntile[:, 4, :], ntile[:, 3, :], float(P), float(N), ALU.mult, ALU.add))
            link(dve.tensor_tensor(place[:, :, :], ps_u[0][:, 0:NT * E].rearrange("p (t e) -> p t e", e=E),
                                   ntile[:, 4, :].rearrange("p (a e) -> p a e", a=1).broadcast_to([P, NT, E]), ALU.add))
            for k in range(TOPK):
                link(dve.tensor_tensor(oh[:, k, :, :], oh[:, k, :, :], place[:, :, :], ALU.mult))
                link(dve.tensor_reduce(slotf[:, k, :], oh[:, k, :, :], AX_X, ALU.add))
            dve.tensor_copy(slot[:, :, :], slotf[:, :, :]).then_inc(s_place, 1)
            ends = big[:, :].rearrange("p (t e) -> p t e", e=E)
            link(dve.tensor_tensor(ends, ntile[:, cur, :].rearrange("p (a e) -> p a e", a=1).broadcast_to([P, TILES, E]),
                                   iota_t[:, :].rearrange("p (t a) -> p t a", a=1).broadcast_to([P, TILES, E]), ALU.is_le))
            link(dve.tensor_reduce(eidf[:, NT:ALL], ends, AX_X, ALU.add))
            link(dve.tensor_scalar(eidf[:, NT:ALL], eidf[:, NT:ALL], float(E - 1), None, ALU.min))
            link(dve.memset(eidf[:, 0:NT], float(E)))
            dve.tensor_copy(eid[:, :], eidf[:, :]).then_inc(s_eid, 1)
            dve.wait_ge(s_eid, 1)

            with dve.Fori(0, PAIRS) as ih:
                i0 = dve.snap(ih * 2)
                for b in range(2):
                    i = i0 + b
                    e = dve.value_load(eid[0:1, bass.ds(i, 1)], min_val=0, max_val=E)
                    dve.tensor_copy(actrow[:, b, :], acts[:, bass.ds(e, 1), :]).then_inc(s_row, 1)
                    dve.wait_ge(s_row, i + 1)
                    dve.wait_ge(s_h, i + 1)
                    dve.tensor_scalar(gg[:, b, :], ps_h[b][:, 0:HID:2], actrow[:, b, 4:5], actrow[:, b, 3:4], ALU.max, ALU.min).then_inc(s_clip, 1)
                    dve.tensor_scalar(uu[:, b, :], ps_h[b][:, 1:HID:2], actrow[:, b, 6:7], actrow[:, b, 5:6], ALU.max, ALU.min).then_inc(s_clip, 1)
                    dve.wait_ge(s_sig, i + 1)
                    dve.wait_ge(s_clip, i * 2 + 2)
                    dve.scalar_tensor_tensor(sg[:, b, :], gg[:, b, :], actrow[:, b, 1:2], sg[:, b, :], ALU.mult, ALU.mult).then_inc(s_row2, 1)
                    dve.wait_ge(s_row2, i + 1)
                    dve.scalar_tensor_tensor(te[:, b, :], uu[:, b, :], actrow[:, b, 2:3], sg[:, b, :], ALU.add, ALU.mult).then_inc(s_te, 1)
            for t in range(NT):
                b = t % 2
                dve.wait_ge(s_yg[b], 16 * (TOPK + 1) * (t // 2 + 1))
                if t >= 2:
                    dve.wait_ge(s_out[b], 16 * (t // 2))
                link(dve.scalar_tensor_tensor(ya[:, b, :], yg[:, b, 0, :], cw[:, 0, t:t + 1], yg[:, b, TOPK, :], ALU.mult, ALU.add))
                dve.scalar_tensor_tensor(ya[:, b, :], yg[:, b, 1, :], cw[:, 1, t:t + 1], ya[:, b, :], ALU.mult, ALU.add).then_inc(s_sum, 1)
                dve.wait_ge(s_sum, t + 1)
                dve.tensor_tensor(ya[:, b, :], ya[:, b, :], xacc[:, t, :], ALU.add).then_inc(s_res, 1)


def graph_attention_and_experts(nc, x, adj, Wks, Wqs, Wvs, Wo, gate_w, gate_b, shared_w1, shared_b1, shared_w2,
                                shared_b2, shared_act, expert_w1, expert_b1, expert_w2, expert_b2, expert_act, out):
    N, D = x.shape
    with ExitStack() as ctx:
        def sem(name):
            return ctx.enter_context(nc.semaphore(name))

        xacc = ctx.enter_context(nc.sbuf_tensor("xacc", [P, N // P, D], F32))
        ident = ctx.enter_context(nc.sbuf_tensor("ident", [P, P], F32))
        attention_block(nc, sem, xacc, ident, x, adj, Wks, Wqs, Wvs, Wo)
        expert_block(nc, sem, xacc, ident, gate_w, gate_b, shared_w1, shared_b1, shared_w2, shared_b2, shared_act,
                     expert_w1, expert_b1, expert_w2, expert_b2, expert_act, out)


_INS = ["x", "adj", "L0_gnn_Wks", "L0_gnn_Wqs", "L0_gnn_Wvs", "L0_gnn_Wo", "L0_ffn_gate_w", "L0_ffn_gate_b",
        "L0_ffn_shared_w1", "L0_ffn_shared_b1", "L0_ffn_shared_w2", "L0_ffn_shared_b2", "L0_ffn_shared_act",
        "L0_ffn_expert_w1", "L0_ffn_expert_b1", "L0_ffn_expert_w2", "L0_ffn_expert_b2", "L0_ffn_expert_act"]
_OUTS = [((2048, 256), "float32")]


def kernel(**inputs):
    import numpy as _np
    import concourse.bacc as _bacc
    from concourse import mybir as _mybir
    from concourse.bass_utils import run_bass_kernel_spmd as _run

    nc = _bacc.Bacc("TRN2", target_bir_lowering=False, num_devices=1)
    arrays, args = {}, []
    for name in _INS:
        a = _np.ascontiguousarray(inputs[name])
        arrays[f"in_{name}_dram"] = a
        args.append(nc.dram_tensor(f"in_{name}_dram", a.shape, _mybir.dt.from_np(a.dtype), kind="ExternalInput").ap())
    for i, (shape, dtype) in enumerate(_OUTS):
        dt = _mybir.dt.from_np(_np.dtype(dtype))
        args.append(nc.dram_tensor(f"out_{i}_dram", shape, dt, kind="ExternalOutput").ap())
    graph_attention_and_experts(nc, *args)
    r = _run(nc, [arrays], core_ids=[0])
    got = tuple(r.results[0][f"out_{i}_dram"] for i in range(len(_OUTS)))
    return got[0]
```

```python
from contextlib import ExitStack

import concourse.bass as bass
from concourse import mybir

ALU = mybir.AluOpType
ACT = mybir.ActivationFunctionType
F32 = mybir.dt.float32
F32R = mybir.dt.float32r
I8 = mybir.dt.int8
U32 = mybir.dt.uint32
I32 = mybir.dt.int32
AX_X = mybir.AxisListType.X

P = 128
MASK_EXP = 53
LN_EPS = 1e-5


def f32(ap):
    return ap.bitcast(F32)


def attention_block(nc, sem, xacc, ident, x, adj, Wks, Wqs, Wvs, Wo, padding):
    N, D = x.shape
    H, _, DK = Wks.shape
    NT = N // P
    J = D // P
    CQ = 512
    TC = CQ // P
    NC = N // CQ
    SLOT_W = 1024
    Q_SCALE = 2.0 ** -MASK_EXP * DK ** -0.5
    EXP_SCALE = 2.0 ** MASK_EXP

    with ExitStack() as ctx:
        def sb(name, shape, dt=F32):
            return ctx.enter_context(nc.sbuf_tensor(name, shape, dt))

        def psum(name, shape, dt=F32):
            return ctx.enter_context(nc.psum_tensor(name, shape, dt))

        mask = sb("mask", [P, NT, N], I8)
        xhT = sb("xhT", [P, J, N], F32R)
        xlT = sb("xlT", [P, J, N], F32R)
        kh = sb("kh", [P, N], F32R)
        kl = sb("kl", [P, N], F32R)
        q = sb("q", [P, 2, CQ], F32R)
        v = sb("v", [P, NT, 2 * DK], F32R)
        pr = sb("pr", [P, 2 * TC, N])
        ph = sb("ph", [P, 3, CQ], F32R)
        pl = sb("pl", [P, 3, CQ], F32R)
        oh = sb("oh", [P, CQ], F32R)
        ol = sb("ol", [P, CQ], F32R)
        raw_qk = sb("raw_qk", [P, J, 4, DK])
        wh = sb("wh", [P, J, 4, DK], F32R)
        wl = sb("wl", [P, J, 4, DK], F32R)
        raw_v = sb("raw_v", [P, NT // 2, DK])
        raw_o = sb("raw_o", [P, D])
        woh = sb("woh", [P, D], F32R)
        wol = sb("wol", [P, D], F32R)
        y = sb("y", [P, 2, D])
        stats = sb("stats", [P, NT, 6])
        mv = sb("mv", [P, NT, 2])
        sd = sb("sd", [P, NT])
        rstd = sb("rstd", [P, NT])
        epsc = sb("epsc", [P, 1])
        mx = sb("mx", [P, 2 * TC, 2])
        nbias = sb("nbias", [P, 2 * TC])
        rsum = sb("rsum", [P, 2, TC])
        rinv = sb("rinv", [P, 2, TC])

        slots = [psum(f"slot{i}", [P, SLOT_W]) for i in range(2)]
        pts = [psum(f"pt{i}", [P, CQ]) for i in range(3)]
        po = psum("po", [P, CQ])

        s_x = [sem(f"s_x{g}") for g in range(N // CQ)]
        s_adj = [sem(f"s_adj{t}") for t in range(N // P)]
        s_mask = sem("s_mask")
        s_ident = sem("s_ident")
        s_stat = sem("s_stat")
        s_sd = sem("s_sd")
        s_xn = sem("s_xn")
        s_lnt = sem("s_lnt")
        s_lnh = sem("s_lnh")
        s_lnl = sem("s_lnl")
        s_rawqk = sem("s_rawqk")
        s_rawwv = sem("s_rawwv")
        s_wv = sem("s_wv")
        s_vall = sem("s_vall")
        s_vcopied = sem("s_vcopied")
        s_vstored = sem("s_vstored")
        s_rawv = sem("s_rawv")
        s_v = sem("s_v")
        s_v_used = sem("s_v_used")
        s_rawo = sem("s_rawo")
        s_wqk = sem("s_wqk")
        s_wo = sem("s_wo")
        s_wqk_used = sem("s_wqk_used")
        s_wo_used = sem("s_wo_used")
        s_slot = sem("s_slot")
        s_hi = sem("s_hi")
        s_free = [sem("s_free0"), sem("s_free1")]
        s_y = sem("s_y")
        s_add = sem("s_add")
        s_max = sem("s_max")
        s_prob = sem("s_prob")
        s_pt = sem("s_pt")
        s_ph = sem("s_ph")
        s_pl = sem("s_pl")
        s_pv = sem("s_pv")
        s_oh = sem("s_oh")
        s_ol = sem("s_ol")
        s_rinv = sem("s_rinv")
        s_tick = sem("s_tick")
        s_diag = sem("s_diag")
        s_pool_tick = sem("s_pool_tick")
        s_zeros = sem("s_zeros")
        s_padding = sem("s_padding")

        LAST = NC * H
        PAIRS = NT // 2
        LAG = 2
        WAYS = 3

        def plan(n):
            c = n % NC
            scores, trans, later = 0 <= n < LAST, 1 <= n <= LAST, n >= 2
            more = n < LAST - 1
            s = [("S", t, half) for t in range(TC) for half in range(2)] if scores else []
            p_ = [("P", k) for k in range(PAIRS)] if trans else []
            out_ = [("Q", 0), ("K", 0), ("K", 1)] if n == 0 else []
            out_ += s[:2]
            if later:
                out_.append(("E",))
            for k in range(PAIRS):
                out_ += p_[k:k + 1]
                out_ += s[k + 2:k + 3]
                if k == 1 and more and scores:
                    out_.append(("Q", (c + 1) % NC))
                if k == 3 and later:
                    out_.append(("W",))
                if c == NC - 1 and more and scores and k in (5, 6):
                    out_.append(("K", k - 5))
            return out_

        def scalar_plan(n):
            out_ = []
            has_pairs = any(it[0] == "P" for it in plan(n))
            for it in plan(n):
                if it[0] == "S":
                    if it[2] == 1 and not has_pairs:
                        out_.append(("X", it[1]))
                    continue
                out_.append(it + (0,) if it[0] == "W" else it)
                if it[0] == "P" and n < LAST and it[1] in (0, 2, 4, 6):
                    out_.append(("X", it[1] // 2))
                if it[0] == "P" and ("W", 0) in out_ and ("W", 1) not in out_:
                    out_.append(("W", 1))
            return out_ + [("W", 1)] * (("W", 0) in out_ and ("W", 1) not in out_)

        SLOT, HI = {}, {}
        for n in range(LAST + 2):
            for it in plan(n):
                for half in range({"Q": 1, "K": 1, "S": 1, "W": 1}.get(it[0], 0)):
                    SLOT[n, it, half] = len(SLOT)
                    if it[0] in "QK":
                        HI[n, it, half] = len(HI)
        FIRST, BODY, LOOPS = 2, NC, H - 1

        def per(d):
            return sum(FIRST <= k[0] < FIRST + BODY for k in d)

        PER = dict(slot=per(SLOT), buf=per(SLOT) // 2, hi=per(HI), kt=BODY * NT, tile=BODY * TC, chunk=BODY, y=2 * BODY, v=4, head=1, head2=2, qk=64, wo=32)
        assert PER["slot"] % 2 == 0 and (FIRST + BODY) % 2 == 0

        def attention(eng, step, keys):
            zero = dict.fromkeys(PER, 0)
            for n in range(FIRST):
                step(n, zero)
            with eng.Fori(0, LOOPS) as i:
                off = {k: eng.snap(i * PER[k]) for k in keys}
                for n in range(FIRST, FIRST + BODY):
                    step(n, off)
            for n in range(FIRST + LOOPS * BODY, LAST + 2):
                step(n, zero)

        block = ctx.enter_context(nc.Block())

        v_all = nc.dram_tensor("v_all", [H, P, NT * DK], F32, kind="Internal").ap()
        v_stage = pr[:, TC:2 * TC, :].rearrange("p a (b t k) -> p (a b) t k", t=NT, k=DK)
        wv_raw = pr[:, 0, N - J * H * DK:N]
        wvh, wvl = kl[:, 0:J * H * DK], kl[:, J * H * DK:2 * J * H * DK]

        def load_qk(eng, h):
            for s_, w in ((0, Wqs), (1, Wqs), (2, Wks), (3, Wks)):
                src = w[bass.ds(h, 1), :, :].rearrange("a (j p) k -> p (a j) k", p=P)
                eng.dma_start(raw_qk[:, :, s_, :], src).then_inc(s_rawqk, 16)

        def load_wo(eng, h):
            for half in range(2):
                eng.dma_start(raw_o[half * DK:(half + 1) * DK, :],
                              Wo[bass.ds(h, 1), :, :].rearrange("a k d -> (a k) d")).then_inc(s_rawo, 16)

        def load_v(eng, h, half):
            cols = slice(half * NT // 2 * DK, (half + 1) * NT // 2 * DK)
            eng.dma_start(raw_v[:, :, :], v_all[bass.ds(h, 1), :, cols].rearrange("a p (t k) -> (a p) t k", k=DK)).then_inc(s_rawv, 16)

        @block.sync
        def _(sp):
            for g in range(NT // TC):
                sp.dma_start(xacc[:, g * TC:(g + 1) * TC, :],
                             x[g * TC * P:(g + 1) * TC * P, :].rearrange("(t p) d -> p t d", p=P)).then_inc(s_x[g], 16)
            for h in range(H):
                sp.dma_start(wv_raw.rearrange("p (j h k) -> p j h k", j=J, h=H)[:, :, h, :],
                             Wvs[h].rearrange("(j p) k -> p j k", p=P)).then_inc(s_rawwv, 16)
            load_qk(sp, 0)
            load_wo(sp, 0)
            sp.wait_ge(s_zeros, 1)
            sp.dma_start(padding.rearrange("(t p) d -> p t d", p=P),
                         y[:, 0:1, :].broadcast_to([P, padding.shape[0] // P, D])).then_inc(s_padding, 16)
            sp.wait_ge(s_vcopied, NT)
            sp.dma_start(v_all.rearrange("h p c -> p h c"), v_stage.rearrange("p h t k -> p h (t k)")).then_inc(s_vstored, 16)
            sp.wait_ge(s_vstored, 16)
            for half in range(2):
                if half:
                    sp.wait_ge(s_v, 2)
                load_v(sp, 0, half)
            with sp.Fori(1, H) as h:
                sp.wait_ge(s_wqk, h * 2)
                load_qk(sp, h)
                sp.wait_ge(s_v, h * 4)
                load_v(sp, h, 0)
                sp.wait_ge(s_wo, h * 2)
                load_wo(sp, h)
                sp.wait_ge(s_v, h * 4 + 2)
                load_v(sp, h, 1)

        @block.gpsimd
        def _(pool):
            pool.memset(ident[:, :], 0.0).then_inc(s_ident, 1)
            pool.wait_ge(s_ident, 1)
            pool.affine_select(out=ident[:, :], in_=ident[:, :], compare_op=ALU.not_equal, fill=1.0, base=0,
                               pattern=[[-1, P]], channel_multiplier=1).then_inc(s_ident, 1)
            pool.memset(y[:, 0, :], 0.0).then_inc(s_zeros, 1)
            for t in range(NT):
                pool.dma_start(mask[:, t, :], adj[t * P:(t + 1) * P, :]).then_inc(s_adj[t], 16)

            def diagonal(t):
                d = mask[:, t, t * P:(t + 1) * P]
                pool.wait_ge(s_adj[t], 16)
                pool.affine_select(out=d, in_=d, compare_op=ALU.not_equal, fill=1.0, base=0,
                                   pattern=[[-1, P]], channel_multiplier=1).then_inc(s_diag, 1)

            def split(high, low, raw, loaded, loads, done, before):
                pool.wait_ge(loaded, loads)
                pool.sem_inc(s_pool_tick)
                pool.tensor_copy(high, raw).then_inc(done, 1)
                pool.wait_ge(done, before + 1)
                pool.tensor_tensor(low, raw, f32(high), ALU.subtract).then_inc(done, 1)

            def split_qk(h, off):
                split(wh[:, :, :, :], wl[:, :, :, :], raw_qk[:, :, :, :], s_rawqk, (h + 1) * 64 + off["qk"], s_wqk, 2 * h + off["head2"])

            def split_wo(h, off):
                split(woh[:, :], wol[:, :], raw_o[:, :], s_rawo, (h + 1) * 32 + off["wo"], s_wo, 2 * h + off["head2"])

            def split_v(h, half, off):
                ts = slice(half * (NT // 2), (half + 1) * (NT // 2))
                split(v[:, ts, 0:DK], v[:, ts, DK:2 * DK], raw_v[:, :, :], s_rawv, (2 * h + half + 1) * 16 + off["wo"],
                      s_v, 4 * h + 2 * half + off["v"])

            split(wvh, wvl, wv_raw, s_rawwv, 16 * H, s_wv, 0)
            zero = dict.fromkeys(PER, 0)
            split_qk(0, zero)
            for t in range(NT):
                diagonal(t)
            split_wo(0, zero)
            split_v(0, 0, zero)
            split_v(0, 1, zero)

            def step(n, off):
                c, h = n % NC, n // NC
                if 2 <= n < LAST:
                    if c == 2 and h < H - 1:
                        pool.wait_ge(s_wqk_used, h + 1 + off["head"])
                        split_qk(h + 1, off)
                    if c == 1:
                        pool.wait_ge(s_pv, n - 1 + off["chunk"])
                        split_v(h, 1, off)
                if n >= 2:
                    m = n - 2
                    for half in range(2):
                        pool.wait_ge(s_y, m * TC + 2 * half + 2 + off["tile"])
                        if m > 0 or half > 0:
                            pool.wait_ge(s_add, m * 2 + half + off["y"])
                        xt = xacc[:, m % NC * TC + 2 * half:m % NC * TC + 2 * half + 2, :]
                        pool.tensor_tensor(xt, xt, y[:, :, :], ALU.add).then_inc(s_add, 1)
                if 2 <= n < LAST:
                    if c == 0:
                        pool.wait_ge(s_v_used, h + off["head"])
                        split_v(h, 0, off)
                    if c == 1:
                        pool.wait_ge(s_wo_used, h + off["head"])
                        split_wo(h, off)

            attention(pool, step, ("tile", "chunk", "y", "v", "head", "head2", "qk", "wo"))

        @block.tensor
        def _(pe):
            pe.wait_ge(s_ident, 2)
            for g in range(NT // TC):
                if g >= 2:
                    pe.wait_ge(s_lnl, g - 1)
                for t in range(TC):
                    pe.wait_ge(s_xn, g * TC + t + 1)
                    for j in range(J):
                        last = pe.transpose(slots[g % 2][:, j * CQ + t * P:j * CQ + (t + 1) * P],
                                            pr[:, g % 2 * TC + t, j * P:(j + 1) * P], ident[:, :])
                last.then_inc(s_lnt, 1)
            pe.wait_ge(s_lnl, NT // TC)
            pe.wait_ge(s_wv, 2)

            def triple(o, lh, ll, rh, rl, first, last):
                pe.matmul(o, lh, rh, start=first, stop=False)
                pe.matmul(o, ll, rh, start=False, stop=False)
                return pe.matmul(o, lh, rl, start=False, stop=last)

            for t in range(NT):
                if t >= 4:
                    pe.wait_ge(s_vcopied, t - 3)
                o = slots[t // 2 % 2][:, t % 2 * H * DK:(t % 2 + 1) * H * DK]
                nodes = slice(t * P, (t + 1) * P)
                for j in range(J):
                    cols = slice(j * H * DK, (j + 1) * H * DK)
                    last = triple(o, xhT[:, j, nodes], xlT[:, j, nodes], wvh[:, cols], wvl[:, cols], j == 0, j == J - 1)
                last.then_inc(s_vall, 1)
            pe.wait_ge(s_vcopied, NT)

            def slot(n, it, half, off):
                k = SLOT[n, it, half]
                if k >= 2:
                    pe.wait_ge(s_free[k % 2], k // 2 + off["buf"])
                return slots[k % 2]

            def slots_read(k, off):
                pe.wait_ge(s_free[k % 2], k // 2 + 1 + off["buf"])

            def times_v(m, kt, off):
                g = m * NT + kt
                if kt == 0 and m >= 1:
                    pe.wait_ge(s_ol, m + off["chunk"])
                if kt % (NT // 2) == 0 and m % NC == 0:
                    pe.wait_ge(s_v, 4 * (m // NC) + 2 + 2 * (kt // (NT // 2)) + off["v"])
                pe.wait_ge(s_pl, g + 1 + off["kt"])
                pe.matmul(po[:, :], v[:, kt, :], ph[:, kt % WAYS, :], start=(kt == 0), stop=False)
                last = pe.matmul(po[:, :], v[:, kt, :], pl[:, kt % WAYS, :], start=False, stop=(kt == NT - 1))
                if kt == NT - 1:
                    last.then_inc(s_pv, 1)
                elif kt == NT // 2 - 1 and m % NC == NC - 1:
                    last.then_inc(s_v_used, 1)

            def step(n, off):
                for it in plan(n):
                    kind = it[0]
                    if kind == "Q":
                        a = it[1]
                        o = slot(n, it, 0, off)
                        if a == 0:
                            pe.wait_ge(s_wqk, 2 * ((n + 1) // NC + 1) + off["head2"])
                        for j in range(J):
                            cols = slice(a * CQ, (a + 1) * CQ)
                            last = triple(o[:, 0:CQ], wh[:, j, 0:2, :], wl[:, j, 0:2, :],
                                          xhT[:, j, cols], xlT[:, j, cols], j == 0, j == J - 1)
                        last.then_inc(s_slot, 1)
                        if a == NC - 1:
                            pe.wait_ge(s_slot, SLOT[n, it, 0] + 1 + off["slot"])
                            pe.sem_inc(s_wqk_used)
                    elif kind == "K":
                        a = it[1]
                        o = slot(n, it, 0, off)
                        for b in range(2):
                            for j in range(J):
                                cols = slice((2 * a + b) * CQ, (2 * a + b + 1) * CQ)
                                last = triple(o[:, b * CQ:(b + 1) * CQ], wh[:, j, 2:4, :], wl[:, j, 2:4, :],
                                              xhT[:, j, cols], xlT[:, j, cols], j == 0, j == J - 1)
                        last.then_inc(s_slot, 1)
                    elif kind == "S":
                        _, t, half = it
                        o = slot(n, it, 0, off)
                        if t == 0 and half == 0:
                            slots_read(SLOT[n, it, 0] - 1, off)
                        qt = q[:, n % 2, t * P:(t + 1) * P]
                        for b in range(2):
                            cols = slice((2 * half + b) * CQ, (2 * half + b + 1) * CQ)
                            pe.matmul(o[:, b * CQ:(b + 1) * CQ], qt, kh[:, cols], start=True, stop=False)
                            last = pe.matmul(o[:, b * CQ:(b + 1) * CQ], qt, kl[:, cols], start=False, stop=True)
                        last.then_inc(s_slot, 1)
                    elif kind == "P":
                        m = n - 1
                        for kt in (2 * it[1], 2 * it[1] + 1):
                            g = m * NT + kt
                            if kt == 0:
                                pe.wait_ge(s_prob, TC * n + off["tile"])
                                if m >= 1:
                                    pe.wait_ge(s_pl, g + off["kt"])
                            elif kt >= WAYS:
                                pe.wait_ge(s_pl, g - WAYS + 1 + off["kt"])
                            for t in range(TC):
                                last = pe.transpose(pts[kt % WAYS][:, t * P:(t + 1) * P],
                                                    pr[:, m % 2 * TC + t, kt * P:(kt + 1) * P], ident[:, :])
                            last.then_inc(s_pt, 1)
                            if kt >= LAG:
                                times_v(m, kt - LAG, off)
                    elif kind == "E":
                        for kt in range(NT - LAG, NT):
                            times_v(n - 2, kt, off)
                    elif kind == "W":
                        m = n - 2
                        o = slot(n, it, 0, off)
                        pe.wait_ge(s_ol, m + 1 + off["chunk"])
                        if m % NC == 0:
                            pe.wait_ge(s_wo, 2 * (m // NC + 1) + off["head2"])
                        for t in range(TC):
                            cols = slice(t * P, (t + 1) * P)
                            last = triple(o[:, t * D:(t + 1) * D], oh[:, cols], ol[:, cols], woh[:, :], wol[:, :], True, True)
                        last.then_inc(s_slot, 1)
                        if m % NC == NC - 1:
                            pe.wait_ge(s_slot, SLOT[n, it, 0] + 1 + off["slot"])
                            pe.sem_inc(s_wo_used)

            attention(pe, step, ("slot", "buf", "kt", "tile", "chunk", "v", "head2"))

        @block.scalar
        def _(act):
            act.wait_ge(s_stat, 2 * NT + 1)
            act.activation(sd[:, :], mv[:, :, 1], ACT.Sqrt, bias=epsc[:, 0:1]).then_inc(s_sd, 1)
            for g in range(NT // TC):
                act.wait_ge(s_lnt, g + 1)
                act.activation(xhT[:, :, g * CQ:(g + 1) * CQ], slots[g % 2][:, :].rearrange("p (j n) -> p j n", j=J),
                               ACT.Copy).then_inc(s_lnh, 1)

            for t in range(NT):
                act.wait_ge(s_vall, t + 1)
                act.activation(v_stage[:, :, t, :], slots[t // 2 % 2][:, t % 2 * H * DK:(t % 2 + 1) * H * DK].rearrange("p (h k) -> p h k", k=DK),
                               ACT.Copy).then_inc(s_vcopied, 1)

            def step(n, off):
                for it in scalar_plan(n):
                    kind = it[0]
                    if kind in ("Q", "K"):
                        k = SLOT[n, it, 0]
                        act.wait_ge(s_slot, k + 1 + off["slot"])
                        o = slots[k % 2]
                        if kind == "Q":
                            m = act.activation(q[:, it[1] % 2, :], o[:, 0:CQ], ACT.Copy, scale=Q_SCALE)
                        else:
                            m = act.activation(kh[:, it[1] * SLOT_W:(it[1] + 1) * SLOT_W], o[:, :], ACT.Copy)
                        m.then_inc(s_hi, 1)
                    elif kind == "X":
                        i = n % 2 * TC + it[1]
                        act.wait_ge(s_max, n * TC + it[1] + 1 + off["tile"])
                        act.activation(pr[:, i, :], pr[:, i, :], ACT.Exp, bias=nbias[:, i:i + 1], scale=EXP_SCALE,
                                       accum_out=rsum[:, n % 2, it[1]:it[1] + 1]).then_inc(s_prob, 1)
                    elif kind == "P":
                        for kt in (2 * it[1], 2 * it[1] + 1):
                            act.wait_ge(s_pt, (n - 1) * NT + kt + 1 + off["kt"])
                            act.activation(ph[:, kt % WAYS, :], pts[kt % WAYS][:, :], ACT.Copy).then_inc(s_ph, 1)
                    elif kind == "E":
                        act.wait_ge(s_pv, n - 1 + off["chunk"])
                        act.activation(oh[:, :], po[:, :], ACT.Copy).then_inc(s_oh, 1)
                    elif kind == "W":
                        m, k, half = n - 2, SLOT[n, ("W",), 0], it[1]
                        act.wait_ge(s_slot, k + 1 + off["slot"])
                        act.wait_ge(s_rinv, m + 1 + off["chunk"])
                        if m == 0 and half == 0:
                            act.wait_ge(s_padding, 16)
                        if m * 2 + half > 0:
                            act.wait_ge(s_add, m * 2 + half + off["y"])
                        for t in (2 * half, 2 * half + 1):
                            act.activation(y[:, t % 2, :], slots[k % 2][:, t * D:(t + 1) * D], ACT.Copy,
                                           scale=rinv[:, m % 2, t:t + 1]).then_inc(s_y, 1)
                        if half == 1:
                            act.wait_ge(s_y, (m + 1) * TC + off["tile"])
                            act.sem_inc(s_free[k % 2])

            attention(act, step, ("slot", "kt", "tile", "chunk", "y"))

        @block.vector
        def _(dve):
            dve.memset(epsc[:, :], LN_EPS).then_inc(s_stat, 1)
            for t in range(NT):
                if t % TC == 0:
                    dve.wait_ge(s_x[t // TC], 16)
                dve.bn_stats(stats[:, t, :], xacc[:, t, :]).then_inc(s_stat, 1)
            for t in range(NT):
                dve.wait_ge(s_stat, t + 2)
                dve.bn_aggr(mv[:, t, :], stats[:, t, :]).then_inc(s_stat, 1)
            dve.wait_ge(s_sd, 1)
            dve.reciprocal(rstd[:, :], sd[:, :]).then_inc(s_stat, 1)
            dve.wait_ge(s_stat, 2 * NT + 2)

            def split_rows(g):
                dve.wait_ge(s_lnh, g + 1)
                dve.tensor_tensor(xlT[:, :, g * CQ:(g + 1) * CQ], slots[g % 2][:, :].rearrange("p (j n) -> p j n", j=J),
                                  f32(xhT[:, :, g * CQ:(g + 1) * CQ]), ALU.subtract).then_inc(s_lnl, 1)

            for g in range(NT // TC):
                for t in range(TC):
                    tt = g * TC + t
                    if g >= 2:
                        dve.wait_ge(s_lnt, g - 1)
                    dve.tensor_scalar(pr[:, g % 2 * TC + t, 0:D], xacc[:, tt, :], mv[:, tt, 0:1], rstd[:, tt:tt + 1],
                                      ALU.subtract, ALU.mult).then_inc(s_xn, 1)
                if g >= 1:
                    split_rows(g - 1)
            split_rows(NT // TC - 1)
            for t in range(NT):
                dve.wait_ge(s_diag, t + 1)
                dve.tensor_scalar(mask[:, t, :], mask[:, t, :], -1.0, None, ALU.add).then_inc(s_mask, 1)
            dve.wait_ge(s_mask, NT)

            def step(n, off):
                for it in plan(n):
                    kind = it[0]
                    if kind in ("Q", "K"):
                        k = SLOT[n, it, 0]
                        dve.wait_ge(s_hi, HI[n, it, 0] + 1 + off["hi"])
                        o = slots[k % 2]
                        if kind == "Q":
                            m = dve.scalar_tensor_tensor(q[DK:P, it[1] % 2, :], o[DK:P, 0:CQ], Q_SCALE,
                                                         f32(q[DK:P, it[1] % 2, :]), ALU.mult, ALU.subtract)
                        else:
                            cols = slice(it[1] * SLOT_W, (it[1] + 1) * SLOT_W)
                            m = dve.tensor_tensor(kl[:, cols], o[:, :], f32(kh[:, cols]), ALU.subtract)
                        m.then_inc(s_free[k % 2], 1)
                    elif kind == "S":
                        _, t, half = it
                        i, qt, k = n % 2 * TC + t, n % NC * TC + t, SLOT[n, it, 0]
                        if n == 1 and t == 0 and half == 0:
                            dve.wait_ge(s_vstored, 16)
                        dve.wait_ge(s_slot, k + 1 + off["slot"])
                        dve.sem_inc(s_tick)
                        cols = slice(half * SLOT_W, (half + 1) * SLOT_W)
                        dve.tensor_tensor_reduce(pr[:, i, cols], slots[k % 2][:, :], mask[:, qt, cols], 1.0, -3.0e38,
                                                 ALU.add, ALU.max, mx[:, i, half:half + 1]).then_inc(s_free[k % 2], 1)
                        if half == 1:
                            for kk in (SLOT[n, ("S", t, 0), 0], k):
                                dve.wait_ge(s_free[kk % 2], kk // 2 + 1 + off["buf"])
                            dve.tensor_scalar(nbias[:, i:i + 1], mx[:, i, 0:1], mx[:, i, 1:2], -EXP_SCALE,
                                              ALU.max, ALU.mult).then_inc(s_max, 1)
                    elif kind == "P":
                        m = n - 1
                        for kt in (2 * it[1], 2 * it[1] + 1):
                            w_ = kt % WAYS
                            dve.wait_ge(s_ph, m * NT + kt + 1 + off["kt"])
                            dve.tensor_tensor(pl[:, w_, :], pts[w_][:, :], f32(ph[:, w_, :]), ALU.subtract).then_inc(s_pl, 1)
                            if kt == 0:
                                dve.reciprocal(rinv[:, m % 2, :], rsum[:, m % 2, :]).then_inc(s_rinv, 1)
                    elif kind == "E":
                        dve.wait_ge(s_oh, n - 1 + off["chunk"])
                        dve.tensor_tensor(ol[:, :], po[:, :], f32(oh[:, :]), ALU.subtract).then_inc(s_ol, 1)

            attention(dve, step, ("slot", "buf", "kt", "chunk", "hi"))


def routed_tiles(N, E):
    tiles = (2 * N + (P - 1) * E) // P
    return tiles + tiles % 2


def expert_block(nc, sem, xacc, ident, xs, gate_w, gate_b, shared_w1, shared_b1, shared_w2, shared_b2, shared_act,
                 expert_w1, expert_b1, expert_w2, expert_b2, expert_act, out):
    D = gate_w.shape[0]
    E = gate_w.shape[1]
    HID = shared_w1.shape[1]
    I = HID // 2
    NT = xacc.shape[1]
    N = NT * P
    J = D // P
    KI = 96
    JI = I // KI
    TOPK = 2
    TILES = routed_tiles(N, E)
    ALL = NT + TILES
    JT = N // P
    NACT = 7

    with ExitStack() as ctx:
        def sb(name, shape, dt=F32):
            return ctx.enter_context(nc.sbuf_tensor(name, shape, dt))

        def psum(name, shape, dt=F32):
            return ctx.enter_context(nc.psum_tensor(name, shape, dt))

        ys = nc.dram_tensor("expert_results", [ALL * P, D], F32, kind="Internal").ap()

        w1 = sb("w1", [P, E + 1, J, HID])
        w2 = sb("w2", [KI, E + 1, JI, D])
        b1 = sb("b1", [P, E + 1, HID])
        b2 = sb("b2", [P, E + 1, D])
        gw = sb("gw", [P, J, E])
        gb = sb("gb", [P, E])
        araw = sb("araw", [P, E + 1, 5])
        acts = sb("acts", [P, E + 1, NACT])
        sp_t = sb("sp_t", [P, 4, E + 1, 2])
        ones = sb("ones", [P, P])
        before = sb("before", [P, P])
        zeros = sb("zeros", [P, D])
        iota_e = sb("iota_e", [P, E])
        iota_t = sb("iota_t", [P, TILES])
        iota_j = sb("iota_j", [P, JT])
        xn = sb("xn2", [P, NT, D])
        stats = sb("stats2", [P, NT, 6])
        mv = sb("mv2", [P, NT, 2])
        sd = sb("sd2", [P, NT])
        rstd = sb("rstd2", [P, NT])
        epsc = sb("epsc2", [P, 1])
        xT = sb("xT", [P, 2, J, P])
        logits = sb("logits", [P, NT, E])
        top = sb("top", [P, NT, 8])
        topi = sb("topi", [P, NT, 8], U32)
        topf = sb("topf", [P, TOPK, NT])
        diff = sb("diff", [P, NT])
        e2 = sb("e2", [P, NT])
        den = sb("den", [P, NT])
        cw = sb("cw", [P, TOPK, NT])
        oh = sb("onehot", [P, TOPK, NT, E])
        oh12 = sb("oh12", [P, NT, E])
        big = sb("big", [P, E * TILES])
        ntile = sb("ntile", [P, 6, E])
        place = sb("place", [P, NT, E])
        slotf = sb("slotf", [P, TOPK, NT])
        slot = sb("slot", [P, TOPK, NT], U32)
        eidf = sb("eidf", [P, ALL])
        eid = sb("eid", [P, ALL], I32)
        xin = sb("xin", [P, 2, D])
        actrow = sb("actrow", [P, 2, NACT])
        hb = sb("hb", [P, 2, HID])
        gg = sb("gg", [P, 2, I])
        uu = sb("uu", [P, 2, I])
        sg = sb("sg", [P, 2, I])
        te = sb("te", [P, 2, I])
        teT = sb("teT", [KI, 2, JI, P])
        yo = sb("yo", [P, 2, D])
        yg = sb("yg", [P, 2, TOPK, D])
        zg = sb("zg", [P, 2, D])
        ya = sb("ya", [P, 2, D])

        ps_t = [psum(f"ps_t{i}", [P, 512]) for i in range(2)]
        ps_h = [psum(f"ps_h{i}", [P, 512]) for i in range(2)]
        ps_u = [psum(f"ps_u{i}", [P, 512]) for i in range(2)]
        ps_y = [psum(f"ps_y{i}", [P, 512]) for i in range(2)]

        s_w = sem("e_weights")
        s_ws = sem("e_shared_weights")
        s_eid0 = sem("e_shared_tiles")
        s_hb = sem("e_hb")
        s_gate = sem("e_gate_weights")
        s_act = sem("e_act_table")
        s_const = sem("e_constants")
        s_ln = sem("e_ln")
        s_lnsd = sem("e_lnsd")
        s_xn = sem("e_xn")
        s_gt = sem("e_gate_transposed")
        s_gx = sem("e_gate_copied")
        s_gl = sem("e_gate_logits")
        s_top = sem("e_top")
        s_exp = sem("e_exp")
        s_oh = sem("e_onehot")
        s_cnt = sem("e_counts")
        s_chain = sem("e_chain")
        s_place = sem("e_place")
        s_eid = sem("e_eid")
        s_sp = sem("e_softplus")
        s_rows = sem("e_rows")
        s_scat = sem("e_scattered")
        s_zero = sem("e_zero")
        s_xin = [sem("e_xin0"), sem("e_xin1")]
        s_xt = sem("e_xt")
        s_xc = sem("e_xc")
        s_h = sem("e_h")
        s_row = sem("e_actrow")
        s_clip = sem("e_clip")
        s_row2 = sem("e_gated")
        s_sig = sem("e_sig")
        s_te = sem("e_te")
        s_tt = sem("e_tt")
        s_tc = sem("e_tc")
        s_y = sem("e_y")
        s_yo = sem("e_yo")
        s_ys = [sem("e_ys0"), sem("e_ys1")]
        s_yg = [sem("e_yg0"), sem("e_yg1")]
        s_zg = [sem("e_zg0"), sem("e_zg1")]
        s_sum = sem("e_sum")
        s_res = sem("e_res")
        s_out = [sem("e_out0"), sem("e_out1")]

        block = ctx.enter_context(nc.Block())
        PAIRS = ALL // 2

        @block.sync
        def _(sp):
            sp.dma_start(gw[:, :, :], gate_w.rearrange("(j p) e -> p j e", p=P)).then_inc(s_gate, 16)
            sp.dma_start(gb[:, :], gate_b.rearrange("(a e) -> a e", a=1).broadcast_to([P, E])).then_inc(s_gate, 16)
            sp.dma_start(araw[:, 0:E, :], expert_act.rearrange("(a e) k -> a e k", a=1).broadcast_to([P, E, 5])).then_inc(s_act, 16)
            sp.dma_start(araw[:, E, :], shared_act.rearrange("(a k) -> a k", a=1).broadcast_to([P, 5])).then_inc(s_act, 16)
            for e, (w1_, b1_, w2_, b2_) in enumerate([(shared_w1, shared_b1, shared_w2, shared_b2)]):
                sp.dma_start(w1[:, E, :, :], w1_.rearrange("(j p) h -> p j h", p=P)).then_inc(s_ws, 16)
                sp.dma_start(w2[:, E, :, :], w2_.rearrange("(j p) d -> p j d", p=KI)).then_inc(s_ws, 16)
                sp.dma_start(b1[:, E, :], b1_.rearrange("(a h) -> a h", a=1).broadcast_to([P, HID])).then_inc(s_ws, 16)
                sp.dma_start(b2[:, E, :], b2_.rearrange("(a h) -> a h", a=1).broadcast_to([P, D])).then_inc(s_ws, 16)
            sp.wait_ge(s_xn, NT)
            sp.dma_start(xs[0:N, :].rearrange("(t p) d -> p t d", p=P), xn[:, :, :]).then_inc(s_rows, 16)
            sp.dma_start(b1[:, 0:E, :], expert_b1.rearrange("(a e) h -> a e h", a=1).broadcast_to([P, E, HID])).then_inc(s_w, 16)
            sp.dma_start(b2[:, 0:E, :], expert_b2.rearrange("(a e) h -> a e h", a=1).broadcast_to([P, E, D])).then_inc(s_w, 16)
            for e in range(E):
                sp.dma_start(w1[:, e, :, :], expert_w1[e].rearrange("(j p) h -> p j h", p=P)).then_inc(s_w, 16)
                sp.dma_start(w2[:, e, :, :], expert_w2[e].rearrange("(j p) d -> p j d", p=KI)).then_inc(s_w, 16)
            sp.wait_ge(s_rows, 16)

            def load(i, b):
                sp.dma_start(xin[:, b, :], xs[bass.ds(i * P, P), :]).then_inc(s_xin[b], 16)

            def load_next(ip):
                for b in range(2):
                    sp.wait_ge(s_xt, ip * 2 + b - 1)
                    load(ip * 2 + b, b)

            for b in range(2):
                load(b, b)
            with sp.Fori(1, NT // 2) as ip:
                load_next(ip)
            sp.wait_ge(s_scat, 16 * TOPK * NT)
            sp.wait_ge(s_eid, 1)
            sp.wait_ge(s_w, 16 * (2 + 2 * E))
            with sp.Fori(NT // 2, PAIRS) as ip:
                load_next(ip)
            sp.wait_ge(s_ys[0], 16 * PAIRS)
            sp.wait_ge(s_ys[1], 16 * PAIRS)
            for t in range(NT):
                b = t % 2
                if t >= 2:
                    sp.wait_ge(s_sum, t - 1)
                sp.dma_start(zg[:, b, :], ys[t * P:(t + 1) * P, :]).then_inc(s_zg[b], 16)
                if t >= 1:
                    sp.wait_ge(s_res, t)
                    sp.dma_start(out[(t - 1) * P:t * P, :], ya[:, (t - 1) % 2, :]).then_inc(s_out[(t - 1) % 2], 16)
            sp.wait_ge(s_res, NT)
            sp.dma_start(out[(NT - 1) * P:N, :], ya[:, (NT - 1) % 2, :]).then_inc(s_out[(NT - 1) % 2], 16)
            for b in range(2):
                sp.wait_ge(s_out[b], 16 * (NT // 2))

        @block.gpsimd
        def _(pool):
            pool.memset(zeros[:, :], 0.0).then_inc(s_const, 1)
            pool.memset(ones[:, :], 1.0).then_inc(s_const, 1)
            pool.memset(before[:, :], 1.0).then_inc(s_const, 1)
            pool.wait_ge(s_const, 3)
            pool.affine_select(out=before[:, :], in_=before[:, :], compare_op=ALU.is_gt, fill=0.0, base=0,
                               pattern=[[1, P]], channel_multiplier=-1).then_inc(s_const, 1)
            pool.iota(iota_e[:, :], [[1, E]], base=0, channel_multiplier=0, allow_small_or_imprecise_dtypes=True).then_inc(s_const, 1)
            pool.iota(iota_t[:, :], [[1, TILES]], base=0, channel_multiplier=0, allow_small_or_imprecise_dtypes=True).then_inc(s_const, 1)
            pool.iota(iota_j[:, :], [[P, JT]], base=0, channel_multiplier=0, allow_small_or_imprecise_dtypes=True).then_inc(s_const, 1)
            pool.wait_ge(s_place, 1)
            for k in range(TOPK):
                for t in range(NT):
                    pool.indirect_dma_start(xs, bass.IndirectOffsetOnAxis(slot[:, k, t:t + 1], 0),
                                            xn[:, t, :], None).then_inc(s_scat, 16)
            with pool.Fori(0, PAIRS) as ip:
                for b in range(2):
                    pool.wait_ge(s_yo, ip * 2 + b + 1)
                    pool.dma_start(ys[bass.ds((ip * 2 + b) * P, P), :], yo[:, b, :]).then_inc(s_ys[b], 16)
            pool.wait_ge(s_ys[0], 16 * PAIRS)
            pool.wait_ge(s_ys[1], 16 * PAIRS)
            for t in range(NT):
                b = t % 2
                if t >= 2:
                    pool.wait_ge(s_sum, t - 1)
                for k in range(TOPK):
                    pool.indirect_dma_start(yg[:, b, k, :], None, ys,
                                            bass.IndirectOffsetOnAxis(slot[:, k, t:t + 1], 0)).then_inc(s_yg[b], 16)

        @block.tensor
        def _(pe):
            pe.wait_ge(s_gate, 32)
            for t in range(NT):
                b = t % 2
                pe.wait_ge(s_xn, t + 1)
                if t >= 2:
                    pe.wait_ge(s_gx, t - 1)
                for j in range(J):
                    last = pe.transpose(ps_t[b][:, j * P:(j + 1) * P], xn[:, t, j * P:(j + 1) * P], ident[:, :])
                last.then_inc(s_gt, 1)
                pe.wait_ge(s_gx, t + 1)
                for j in range(J):
                    last = pe.matmul(ps_h[0][:, t * E:(t + 1) * E], xT[:, b, j, :], gw[:, j, :], start=(j == 0), stop=(j == J - 1))
                last.then_inc(s_gl, 1)
            pe.wait_ge(s_oh, 1)
            pe.wait_ge(s_const, 4)
            pe.matmul(ps_u[0][:, 0:NT * E], before[:, :], oh12[:, :, :], start=True, stop=False)
            for t in range(NT - 1):
                rest = NT - 1 - t
                pe.matmul(ps_u[0][:, (t + 1) * E:NT * E], ones[:, :],
                          oh12[:, t:t + 1, :].broadcast_to([P, rest, E]), start=False, stop=(t == NT - 2))
            for t in range(NT):
                last = pe.matmul(ps_u[1][:, 0:E], ones[:, :], oh12[:, t, :], start=(t == 0), stop=(t == NT - 1))
            last.then_inc(s_cnt, 1)

            pe.wait_ge(s_ws, 64)
            pe.wait_ge(s_eid0, 1)

            def stage(base, k):
                b = k % 2

                def there(back):
                    return not isinstance(base, int) or 0 <= base + k - back < ALL

                if there(0):
                    i = base + k
                    pe.wait_ge(s_xin[b], loads(base, k))
                    for j in range(J):
                        last = pe.transpose(ps_t[b][:, j * P:(j + 1) * P], xin[:, b, j * P:(j + 1) * P], ident[:, :])
                    last.then_inc(s_xt, 1)
                if there(1):
                    i, b1_ = base + (k - 1), (k - 1) % 2
                    e = pe.value_load(eid[0:1, bass.ds(i, 1)], min_val=0, max_val=E)
                    pe.wait_ge(s_xc, i + 1)
                    for j in range(J):
                        last = pe.matmul(ps_h[b1_][:, 0:HID], xT[:, b1_, j, :], w1[:, bass.ds(e, 1), j, :],
                                         start=(j == 0), stop=(j == J - 1))
                    last.then_inc(s_h, 1)
                if there(2):
                    i = base + (k - 2)
                    pe.wait_ge(s_te, i + 1)
                    for j in range(JI):
                        last = pe.transpose(ps_u[b][0:KI, j * P:(j + 1) * P], te[:, b, j * KI:(j + 1) * KI], ident[:, :])
                    last.then_inc(s_tt, 1)
                if there(3):
                    i, b3 = base + (k - 3), (k - 3) % 2
                    e = pe.value_load(eid[0:1, bass.ds(i, 1)], min_val=0, max_val=E)
                    pe.wait_ge(s_tc, i + 1)
                    if not isinstance(i, int) or i >= 2:
                        pe.wait_ge(s_yo, i - 1)
                    for j in range(JI):
                        last = pe.matmul(ps_y[b3][:, 0:D], teT[:, b3, j, :], w2[:, bass.ds(e, 1), j, :],
                                         start=(j == 0), stop=(j == JI - 1))
                    last.then_inc(s_y, 1)

            def loads(base, k):
                return 16 * ((base + k) // 2 + 1) if isinstance(base, int) else half_base * 16 + 16 * (k // 2 + 1)

            for k in range(4):
                stage(0, k)
            with pe.Fori(2, PAIRS) as half_base:
                base = pe.snap(half_base * 2)
                for k in range(2):
                    stage(base, k)
            for k in range(3):
                stage(ALL, k)

        @block.scalar
        def _(act):
            act.wait_ge(s_ln, 2 * NT + 1)
            act.activation(sd[:, :], mv[:, :, 1], ACT.Sqrt, bias=epsc[:, 0:1]).then_inc(s_lnsd, 1)
            act.wait_ge(s_sp, 3)
            act.activation(sp_t[:, 2, :, :], sp_t[:, 1, :, :], ACT.Exp, scale=-1.0).then_inc(s_sp, 1)
            act.wait_ge(s_sp, 4)
            act.activation(sp_t[:, 3, :, :], sp_t[:, 2, :, :], ACT.Ln, bias=1.0).then_inc(s_sp, 1)
            for t in range(NT):
                act.wait_ge(s_gt, t + 1)
                if t >= 2:
                    act.wait_ge(s_gl, t - 1)
                act.activation(xT[:, t % 2, :, :], ps_t[t % 2][:, 0:J * P], ACT.Copy).then_inc(s_gx, 1)
            act.wait_ge(s_top, 1)
            act.activation(e2[:, :], diff[:, :], ACT.Exp).then_inc(s_exp, 1)
            act.wait_ge(s_gl, NT)

            def stage(base, k):
                b = k % 2

                def there(back):
                    return not isinstance(base, int) or 0 <= base + k - back < ALL

                if there(0):
                    act.wait_ge(s_xt, base + (k + 1))
                    act.activation(xT[:, b, :, :], ps_t[b][:, 0:J * P], ACT.Copy).then_inc(s_xc, 1)
                if there(2):
                    act.wait_ge(s_tt, base + (k - 1))
                    act.activation(teT[:, b, :, :], ps_u[b][0:KI, 0:JI * P], ACT.Copy).then_inc(s_tc, 1)
                if there(1):
                    b1_ = (k - 1) % 2
                    act.wait_ge(s_clip, base * 2 + (2 * k - 1))
                    act.activation(sg[:, b1_, :], gg[:, b1_, :], ACT.Sigmoid, scale=actrow[:, b1_, 0:1]).then_inc(s_sig, 1)

            for k in range(4):
                stage(0, k)
            with act.Fori(2, PAIRS) as half_base:
                base = act.snap(half_base * 2)
                for k in range(2):
                    stage(base, k)
            for k in range(3):
                stage(ALL, k)

        @block.vector
        def _(dve):
            chain = [0]

            def link(ins):
                chain[0] += 1
                ins.then_inc(s_chain, 1)
                dve.wait_ge(s_chain, chain[0])

            dve.memset(epsc[:, :], LN_EPS).then_inc(s_ln, 1)
            link(dve.memset(eidf[:, 0:NT], float(E)))
            dve.tensor_copy(eid[:, 0:NT], eidf[:, 0:NT]).then_inc(s_eid0, 1)
            for t in range(NT):
                dve.bn_stats(stats[:, t, :], xacc[:, t, :]).then_inc(s_ln, 1)
            for t in range(NT):
                dve.wait_ge(s_ln, t + 2)
                dve.bn_aggr(mv[:, t, :], stats[:, t, :]).then_inc(s_ln, 1)
            dve.wait_ge(s_lnsd, 1)
            link(dve.reciprocal(rstd[:, :], sd[:, :]))
            for t in range(NT):
                dve.tensor_scalar(xn[:, t, :], xacc[:, t, :], mv[:, t, 0:1], rstd[:, t:t + 1],
                                  ALU.subtract, ALU.mult).then_inc(s_xn, 1)
            dve.wait_ge(s_act, 32)
            raw = araw[:, :, 3:5]
            dve.tensor_scalar(sp_t[:, 0, :, :], raw, -1.0, None, ALU.mult).then_inc(s_sp, 1)
            dve.wait_ge(s_sp, 1)
            dve.tensor_tensor(sp_t[:, 1, :, :], raw, sp_t[:, 0, :, :], ALU.max).then_inc(s_sp, 1)
            dve.wait_ge(s_sp, 2)
            dve.tensor_scalar(sp_t[:, 0, :, :], raw, 0.0, None, ALU.max).then_inc(s_sp, 1)
            dve.wait_ge(s_sp, 5)
            link(dve.tensor_tensor(acts[:, :, 3:7:2], sp_t[:, 0, :, :], sp_t[:, 3, :, :], ALU.add))
            link(dve.tensor_scalar(acts[:, :, 4:7:2], acts[:, :, 3:7:2], -1.0, None, ALU.mult))
            link(dve.tensor_copy(acts[:, :, 0:3], araw[:, :, 0:3]))
            dve.wait_ge(s_gl, NT)
            link(dve.tensor_tensor(logits[:, :, :], ps_h[0][:, 0:NT * E].rearrange("p (t e) -> p t e", e=E),
                                   gb[:, :].rearrange("p (a e) -> p a e", a=1).broadcast_to([P, NT, E]), ALU.add))
            for t in range(NT):
                dve.max(top[:, t, :], logits[:, t, :]).then_inc(s_chain, 1)
            chain[0] += NT
            dve.wait_ge(s_chain, chain[0])
            for t in range(NT):
                dve.max_index(topi[:, t, :], top[:, t, :], logits[:, t, :]).then_inc(s_chain, 1)
            chain[0] += NT
            dve.wait_ge(s_chain, chain[0])
            dve.tensor_tensor(diff[:, :], top[:, :, 1], top[:, :, 0], ALU.subtract).then_inc(s_top, 1)
            link(dve.tensor_copy(topf[:, :, :].rearrange("p k t -> p t k"), topi[:, :, 0:TOPK]))
            dve.wait_ge(s_const, 7)
            for k in range(TOPK):
                link(dve.tensor_tensor(oh[:, k, :, :], topf[:, k, :].rearrange("p (t a) -> p t a", a=1).broadcast_to([P, NT, E]),
                                       iota_e[:, :].rearrange("p (a e) -> p a e", a=1).broadcast_to([P, NT, E]), ALU.is_equal))
            dve.tensor_tensor(oh12[:, :, :], oh[:, 0, :, :], oh[:, 1, :, :], ALU.add).then_inc(s_oh, 1)
            dve.wait_ge(s_exp, 1)
            link(dve.tensor_scalar(den[:, :], e2[:, :], 1.0, None, ALU.add))
            link(dve.reciprocal(cw[:, 0, :], den[:, :]))
            link(dve.tensor_tensor(cw[:, 1, :], cw[:, 0, :], e2[:, :], ALU.mult))
            dve.wait_ge(s_cnt, 1)
            cnt = ntile[:, 5, :]
            link(dve.tensor_copy(cnt, ps_u[1][:, 0:E]))
            cmp = big[:, 0:E * JT].rearrange("p (e j) -> p e j", j=JT)
            link(dve.tensor_tensor(cmp, cnt.rearrange("p (e a) -> p e a", a=1).broadcast_to([P, E, JT]),
                                   iota_j[:, :].rearrange("p (a j) -> p a j", a=1).broadcast_to([P, E, JT]), ALU.is_gt))
            link(dve.tensor_reduce(ntile[:, 0, :], cmp, AX_X, ALU.add))
            link(dve.tensor_copy(ntile[:, 1, :], ntile[:, 0, :]))
            cur, step = 1, 1
            while step < E:
                link(dve.tensor_copy(ntile[:, 3 - cur, 0:step], ntile[:, cur, 0:step]))
                link(dve.tensor_tensor(ntile[:, 3 - cur, step:E], ntile[:, cur, step:E], ntile[:, cur, 0:E - step], ALU.add))
                cur, step = 3 - cur, 2 * step
            link(dve.tensor_tensor(ntile[:, 3, :], ntile[:, cur, :], ntile[:, 0, :], ALU.subtract))
            link(dve.tensor_scalar(ntile[:, 4, :], ntile[:, 3, :], float(P), float(N), ALU.mult, ALU.add))
            link(dve.tensor_tensor(place[:, :, :], ps_u[0][:, 0:NT * E].rearrange("p (t e) -> p t e", e=E),
                                   ntile[:, 4, :].rearrange("p (a e) -> p a e", a=1).broadcast_to([P, NT, E]), ALU.add))
            for k in range(TOPK):
                link(dve.tensor_tensor(oh[:, k, :, :], oh[:, k, :, :], place[:, :, :], ALU.mult))
                link(dve.tensor_reduce(slotf[:, k, :], oh[:, k, :, :], AX_X, ALU.add))
            dve.tensor_copy(slot[:, :, :], slotf[:, :, :]).then_inc(s_place, 1)
            ends = big[:, :].rearrange("p (t e) -> p t e", e=E)
            link(dve.tensor_tensor(ends, ntile[:, cur, :].rearrange("p (a e) -> p a e", a=1).broadcast_to([P, TILES, E]),
                                   iota_t[:, :].rearrange("p (t a) -> p t a", a=1).broadcast_to([P, TILES, E]), ALU.is_le))
            link(dve.tensor_reduce(eidf[:, NT:ALL], ends, AX_X, ALU.add))
            link(dve.tensor_scalar(eidf[:, NT:ALL], eidf[:, NT:ALL], float(E - 1), None, ALU.min))
            dve.tensor_copy(eid[:, NT:ALL], eidf[:, NT:ALL]).then_inc(s_eid, 1)

            def stage(base, k):
                def there(back):
                    return not isinstance(base, int) or 0 <= base + k - back < ALL

                if there(1):
                    i, b = base + (k - 1), (k - 1) % 2
                    dve.wait_ge(s_h, i + 1)
                    e = dve.value_load(eid[0:1, bass.ds(i, 1)], min_val=0, max_val=E)
                    dve.tensor_tensor(hb[:, b, :], ps_h[b][:, 0:HID], b1[:, bass.ds(e, 1), :].rearrange("p a h -> p (a h)"), ALU.add).then_inc(s_hb, 1)
                    dve.tensor_copy(actrow[:, b, :], acts[:, bass.ds(e, 1), :].rearrange("p a h -> p (a h)")).then_inc(s_row, 1)
                    dve.wait_ge(s_row, i + 1)
                    dve.tensor_scalar(gg[:, b, :], hb[:, b, 0:HID:2], actrow[:, b, 4:5], actrow[:, b, 3:4], ALU.max, ALU.min).then_inc(s_clip, 1)
                    dve.tensor_scalar(uu[:, b, :], hb[:, b, 1:HID:2], actrow[:, b, 6:7], actrow[:, b, 5:6], ALU.max, ALU.min).then_inc(s_clip, 1)
                if there(3):
                    i3, b3 = base + (k - 3), (k - 3) % 2
                    dve.wait_ge(s_y, i3 + 1)
                    if not isinstance(i3, int) or i3 >= 2:
                        dve.wait_ge(s_ys[b3], stored(base, k - 3))
                    e = dve.value_load(eid[0:1, bass.ds(i3, 1)], min_val=0, max_val=E)
                    dve.tensor_tensor(yo[:, b3, :], ps_y[b3][:, 0:D], b2[:, bass.ds(e, 1), :].rearrange("p a h -> p (a h)"), ALU.add).then_inc(s_yo, 1)
                if there(1):
                    dve.wait_ge(s_sig, i + 1)
                    dve.scalar_tensor_tensor(sg[:, b, :], gg[:, b, :], actrow[:, b, 1:2], sg[:, b, :], ALU.mult, ALU.mult).then_inc(s_row2, 1)
                    dve.wait_ge(s_row2, i + 1)
                    dve.scalar_tensor_tensor(te[:, b, :], uu[:, b, :], actrow[:, b, 2:3], sg[:, b, :], ALU.add, ALU.mult).then_inc(s_te, 1)

            def stored(base, k):
                return 16 * ((base + k) // 2) if isinstance(base, int) else half_base * 16 + 16 * (k // 2)

            for k in range(4):
                stage(0, k)
            with dve.Fori(2, PAIRS) as half_base:
                base = dve.snap(half_base * 2)
                for k in range(2):
                    stage(base, k)
            for k in range(3):
                stage(ALL, k)
            for t in range(NT):
                b = t % 2
                dve.wait_ge(s_yg[b], 16 * TOPK * (t // 2 + 1))
                dve.wait_ge(s_zg[b], 16 * (t // 2 + 1))
                if t >= 2:
                    dve.wait_ge(s_out[b], 16 * (t // 2))
                link(dve.scalar_tensor_tensor(ya[:, b, :], yg[:, b, 0, :], cw[:, 0, t:t + 1], zg[:, b, :], ALU.mult, ALU.add))
                dve.scalar_tensor_tensor(ya[:, b, :], yg[:, b, 1, :], cw[:, 1, t:t + 1], ya[:, b, :], ALU.mult, ALU.add).then_inc(s_sum, 1)
                dve.wait_ge(s_sum, t + 1)
                dve.tensor_tensor(ya[:, b, :], ya[:, b, :], xacc[:, t, :], ALU.add).then_inc(s_res, 1)


def graph_attention_and_experts(nc, x, adj, Wks, Wqs, Wvs, Wo, gate_w, gate_b, shared_w1, shared_b1, shared_w2,
                                shared_b2, shared_act, expert_w1, expert_b1, expert_w2, expert_b2, expert_act, out):
    N, D = x.shape
    with ExitStack() as ctx:
        def sem(name):
            return ctx.enter_context(nc.semaphore(name))

        xacc = ctx.enter_context(nc.sbuf_tensor("xacc", [P, N // P, D], F32))
        ident = ctx.enter_context(nc.sbuf_tensor("ident", [P, P], F32))
        rows = nc.dram_tensor("expert_rows", [N + routed_tiles(N, gate_w.shape[1]) * P, D], F32, kind="Internal").ap()
        attention_block(nc, sem, xacc, ident, x, adj, Wks, Wqs, Wvs, Wo, rows[N:, :])
        expert_block(nc, sem, xacc, ident, rows, gate_w, gate_b, shared_w1, shared_b1, shared_w2, shared_b2, shared_act,
                     expert_w1, expert_b1, expert_w2, expert_b2, expert_act, out)


_INS = ["x", "adj", "L0_gnn_Wks", "L0_gnn_Wqs", "L0_gnn_Wvs", "L0_gnn_Wo", "L0_ffn_gate_w", "L0_ffn_gate_b",
        "L0_ffn_shared_w1", "L0_ffn_shared_b1", "L0_ffn_shared_w2", "L0_ffn_shared_b2", "L0_ffn_shared_act",
        "L0_ffn_expert_w1", "L0_ffn_expert_b1", "L0_ffn_expert_w2", "L0_ffn_expert_b2", "L0_ffn_expert_act"]
_OUTS = [((2048, 256), "float32")]


def kernel(**inputs):
    import numpy as _np
    import concourse.bacc as _bacc
    from concourse import mybir as _mybir
    from concourse.bass_utils import run_bass_kernel_spmd as _run

    nc = _bacc.Bacc("TRN2", target_bir_lowering=False, num_devices=1)
    arrays, args = {}, []
    for name in _INS:
        a = _np.ascontiguousarray(inputs[name])
        arrays[f"in_{name}_dram"] = a
        args.append(nc.dram_tensor(f"in_{name}_dram", a.shape, _mybir.dt.from_np(a.dtype), kind="ExternalInput").ap())
    for i, (shape, dtype) in enumerate(_OUTS):
        dt = _mybir.dt.from_np(_np.dtype(dtype))
        args.append(nc.dram_tensor(f"out_{i}_dram", shape, dt, kind="ExternalOutput").ap())
    graph_attention_and_experts(nc, *args)
    r = _run(nc, [arrays], core_ids=[0])
    got = tuple(r.results[0][f"out_{i}_dram"] for i in range(len(_OUTS)))
    return got[0]
```

```python
from contextlib import ExitStack

import concourse.bass as bass
from concourse import mybir

ALU = mybir.AluOpType
ACT = mybir.ActivationFunctionType
F32 = mybir.dt.float32
F32R = mybir.dt.float32r
I8 = mybir.dt.int8
U32 = mybir.dt.uint32
I32 = mybir.dt.int32
AX_X = mybir.AxisListType.X

P = 128
MASK_EXP = 53
LN_EPS = 1e-5


def f32(ap):
    return ap.bitcast(F32)


def attention_block(nc, sem, xacc, stats, mv, ident, x, adj, Wks, Wqs, Wvs, Wo, rows):
    N, D = x.shape
    H, _, DK = Wks.shape
    NT = N // P
    J = D // P
    CQ = 512
    TC = CQ // P
    NC = N // CQ
    SLOT_W = 1024
    RING = 4
    Q_SCALE = 2.0 ** -MASK_EXP * DK ** -0.5
    EXP_SCALE = 2.0 ** MASK_EXP

    with ExitStack() as ctx:
        def sb(name, shape, dt=F32):
            return ctx.enter_context(nc.sbuf_tensor(name, shape, dt))

        def psum(name, shape, dt=F32):
            return ctx.enter_context(nc.psum_tensor(name, shape, dt))

        mask = sb("mask", [P, NT, N], I8)
        xhT = sb("xhT", [P, J, N], F32R)
        xlT = sb("xlT", [P, J, N], F32R)
        kh = sb("kh", [P, N], F32R)
        kl = sb("kl", [P, N], F32R)
        q = sb("q", [P, N], F32R)
        v = sb("v", [P, NT, 2 * DK], F32R)
        pr = sb("pr", [P, 2 * TC, N])
        ph = sb("ph", [P, RING, CQ], F32R)
        pl = sb("pl", [P, RING, CQ], F32R)
        oh = sb("oh", [P, CQ], F32R)
        ol = sb("ol", [P, CQ], F32R)
        raw_qk = sb("raw_qk", [P, J, 2, DK])
        wh = sb("wh", [P, J, 2, DK], F32R)
        wl = sb("wl", [P, J, 2, DK], F32R)
        raw_v = sb("raw_v", [P, NT // 2, DK])
        raw_o = sb("raw_o", [P, D])
        woh = sb("woh", [P, D], F32R)
        wol = sb("wol", [P, D], F32R)
        y = sb("y", [P, 2, D])
        sd = sb("sd", [P, NT])
        rstd = sb("rstd", [P, NT])
        epsc = sb("epsc", [P, 1])
        mx = sb("mx", [P, 2 * TC, 2])
        nbias = sb("nbias", [P, 2 * TC])
        rsum = sb("rsum", [P, 2, 2, TC])
        rinv = sb("rinv", [P, 2, TC])

        slots = [psum(f"slot{i}", [P, SLOT_W]) for i in range(2)]
        pts = [psum(f"pt{i}", [P, CQ]) for i in range(3)]
        po = psum("po", [P, CQ])

        s_x = [sem(f"s_x{g}") for g in range(N // CQ)]
        s_adj = [sem(f"s_adj{g}") for g in range(N // CQ)]
        s_mask = sem("s_mask")
        s_ident = sem("s_ident")
        s_stat = sem("s_stat")
        s_sd = sem("s_sd")
        s_xn = sem("s_xn")
        s_lnt = sem("s_lnt")
        s_lnh = sem("s_lnh")
        s_lnl = sem("s_lnl")
        s_rawqk = sem("s_rawqk")
        s_rawwv = sem("s_rawwv")
        s_wv = sem("s_wv")
        s_vall = sem("s_vall")
        s_vcopied = sem("s_vcopied")
        s_vstored = sem("s_vstored")
        s_rawv = sem("s_rawv")
        s_v = sem("s_v")
        s_v_used = sem("s_v_used")
        s_rawo = sem("s_rawo")
        s_wqk = sem("s_wqk")
        s_wo = sem("s_wo")
        s_wqk_used = sem("s_wqk_used")
        s_wo_used = sem("s_wo_used")
        s_slot = sem("s_slot")
        s_hi = sem("s_hi")
        s_kl = sem("s_kl")
        s_copied = sem("s_copied")
        s_free = [sem("s_free0"), sem("s_free1")]
        s_y = sem("s_y")
        s_add = sem("s_add")
        s_max = sem("s_max")
        s_prob = sem("s_prob")
        s_pt = sem("s_pt")
        s_ph = sem("s_ph")
        s_pl = sem("s_pl")
        s_pv = sem("s_pv")
        s_oh = sem("s_oh")
        s_ol = sem("s_ol")
        s_rinv = sem("s_rinv")
        s_rsum = sem("s_rsum")
        s_tick = sem("s_tick")
        s_diag = sem("s_diag")
        s_pool_tick = sem("s_pool_tick")
        s_zeros = sem("s_zeros")
        s_rows_zero = sem("s_rows_zero")

        LAST = NC * H
        PAIRS = NT // 2
        LAG = 3
        WAYS = 3

        def is_late(n):
            return n == 1 or 0 < n < LAST and n % NC == 0

        def plan(n):
            c = n % NC
            scores, trans, later = 0 <= n < LAST, 1 <= n <= LAST, n >= 2
            more = n < LAST - 1
            s = [("S", t, half) for t in range(TC) for half in range(2)] if scores else []
            p_ = [("P", k) for k in range(PAIRS)] if trans else []
            if n == 0:
                out_, t = [("K", 0), ("K", 1)], 0
                for it, after in zip([None] + s, (4, 2, 2, 2, 2, 1, 1, 0, 2)):
                    out_ += ([it] if it else []) + [("V", t + i) for i in range(after)]
                    t += after
                assert t == NT
                return out_
            lead = 0 if is_late(n) else 2
            out_ = s[:lead]
            if later:
                out_.append(("E",))
            for k in range(PAIRS):
                out_ += p_[k:k + 1]
                out_ += s[:2 * k] if is_late(n) and k < 2 else s[k + lead:k + lead + 1]
                if k == 2 and later:
                    out_.append(("W",))
                if c == NC - 1 and more and scores and k in (6, 7):
                    out_.append(("K", k - 6))
            return out_

        def scalar_plan(n):
            out_, scored = [], []
            for it in plan(n):
                if it[0] == "S":
                    if n == 0 and it[2] == 1:
                        scored += [("X", it[1], 0), ("X", it[1], 1)]
                    continue
                if it[0] == "V":
                    out_.append(it)
                    out_, scored = out_ + scored[:1], scored[1:]
                    continue
                out_, scored = out_ + scored, []
                out_.append(it + (0,) if it[0] == "W" else it)
                if it[0] == "P" and n < LAST and it[1] >= 2 * is_late(n):
                    at = it[1] - 2 * is_late(n)
                    out_.append(("X", at // 2, at % 2))
                if it[0] == "P" and ("W", 0) in out_ and ("W", 1) not in out_:
                    out_.append(("W", 1))
            out_ += scored + ([("X", TC - 1, 0), ("X", TC - 1, 1)] if is_late(n) else [])
            return out_ + [("W", 1)] * (("W", 0) in out_ and ("W", 1) not in out_)

        SLOT, HI = {}, {}
        for n in range(LAST + 2):
            for it in plan(n):
                for half in range({"K": 1, "S": 1, "W": 1}.get(it[0], 0)):
                    SLOT[n, it, half] = len(SLOT)
                    if it[0] == "K":
                        HI[n, it, half] = len(HI)
        FIRST, BODY, LOOPS = 2, NC, H - 1

        def per(d):
            return sum(FIRST <= k[0] < FIRST + BODY for k in d)

        PER = dict(copies=64, half_tile=2 * BODY * TC, slot=per(SLOT), buf=per(SLOT) // 2, hi=per(HI),
                   two_hi=2 * per(HI), kt=BODY * NT, tile=BODY * TC, chunk=BODY, y=2 * BODY, v=4, head=1,
                   head2=2, qk=32, wo=32)
        LAST_K = {(h, a): (max(NC * h - 1, 0), ("K", a), 0) for h in range(2) for a in range(2)}
        assert PER["slot"] % 2 == 0 and (FIRST + BODY) % 2 == 0

        def attention(eng, step, keys):
            zero = dict.fromkeys(PER, 0)
            for n in range(FIRST):
                step(n, zero)
            with eng.Fori(0, LOOPS) as i:
                off = {k: eng.snap(i * PER[k]) for k in keys}
                for n in range(FIRST, FIRST + BODY):
                    step(n, off)
            for n in range(FIRST + LOOPS * BODY, LAST + 2):
                step(n, zero)

        block = ctx.enter_context(nc.Block())

        v_all = nc.dram_tensor("v_all", [H, P, NT * DK], F32, kind="Internal").ap()
        v_stage = pr[:, TC:2 * TC, :].rearrange("p a (b t k) -> p (a b) t k", t=NT, k=DK)
        wv_raw = pr[:, TC, N - J * H * DK:N]
        wvh, wvl = (ph[:, i * RING // 2:(i + 1) * RING // 2, :].rearrange("p a n -> p (a n)") for i in range(2))

        def load_qk(eng, h):
            for s_, w in enumerate((Wqs, Wks)):
                src = w[bass.ds(h, 1), :, :].rearrange("a (j p) k -> p (a j) k", p=P)
                eng.dma_start(raw_qk[:, :, s_, :], src).then_inc(s_rawqk, 16)

        def load_wo(eng, h):
            for half in range(2):
                eng.dma_start(raw_o[half * DK:(half + 1) * DK, :],
                              Wo[bass.ds(h, 1), :, :].rearrange("a k d -> (a k) d")).then_inc(s_rawo, 16)

        def load_v(eng, h, half):
            cols = slice(half * NT // 2 * DK, (half + 1) * NT // 2 * DK)
            eng.dma_start(raw_v[:, :, :], v_all[bass.ds(h, 1), :, cols].rearrange("a p (t k) -> (a p) t k", k=DK)).then_inc(s_rawv, 16)

        @block.sync
        def _(sp):
            for g in range(NT // TC):
                sp.dma_start(xacc[:, g * TC:(g + 1) * TC, :],
                             x[g * TC * P:(g + 1) * TC * P, :].rearrange("(t p) d -> p t d", p=P)).then_inc(s_x[g], 16)
            def copy_k(h, a):
                last_k = LAST_K[0 if isinstance(h, int) else 1, a]
                turn = 0 if isinstance(h, int) else h - 1
                cols = slice(a * SLOT_W, (a + 1) * SLOT_W)
                for part in (kh, kl):
                    if part is kh:
                        sp.wait_ge(s_hi, 2 * HI[last_k] + 1 + turn * 2 * PER["hi"])
                    else:
                        sp.wait_ge(s_kl, HI[last_k] + 1 + turn * PER["hi"])
                    sp.dma_start(f32(part[0:DK, cols]), f32(part[DK:P, cols])).then_inc(s_copied, 16)

            load_qk(sp, 0)
            for h in range(H):
                sp.dma_start(wv_raw.rearrange("p (j h k) -> p j h k", j=J, h=H)[:, :, h, :],
                             Wvs[h].rearrange("(j p) k -> p j k", p=P)).then_inc(s_rawwv, 16)
            load_wo(sp, 0)
            for a in range(2):
                copy_k(0, a)
            sp.wait_ge(s_zeros, 1)
            sp.dma_start(rows.rearrange("(t p) d -> p t d", p=P),
                         y[:, 0:1, :].broadcast_to([P, rows.shape[0] // P, D])).then_inc(s_rows_zero, 16)
            for g in range(NT // TC):
                sp.wait_ge(s_vcopied, (g + 1) * TC)
                sp.dma_start(v_all[:, :, g * TC * DK:(g + 1) * TC * DK].rearrange("h p c -> p h c"),
                             v_stage[:, :, g * TC:(g + 1) * TC, :].rearrange("p h t k -> p h (t k)")).then_inc(s_vstored, 16)
            sp.wait_ge(s_vstored, 16 * (NT // TC))
            with sp.Fori(1, H) as h:
                sp.wait_ge(s_wqk, h * 2)
                load_qk(sp, h)
                sp.wait_ge(s_v, h * 4)
                load_v(sp, h, 0)
                sp.wait_ge(s_wo, h * 2)
                load_wo(sp, h)
                for a in range(2):
                    copy_k(h, a)
                sp.wait_ge(s_v, h * 4 + 2)
                load_v(sp, h, 1)

        @block.gpsimd
        def _(pool):
            pool.memset(ident[:, :], 0.0).then_inc(s_ident, 1)
            pool.wait_ge(s_ident, 1)
            pool.affine_select(out=ident[:, :], in_=ident[:, :], compare_op=ALU.not_equal, fill=1.0, base=0,
                               pattern=[[-1, P]], channel_multiplier=1).then_inc(s_ident, 1)
            pool.memset(y[:, 0, :], 0.0).then_inc(s_zeros, 1)
            for g in range(NT // TC):
                pool.wait_ge(s_x[g], 16)
            for g in range(NT // TC):
                pool.dma_start(mask[:, g * TC:(g + 1) * TC, :],
                               adj[g * CQ:(g + 1) * CQ, :].rearrange("(t p) n -> p t n", p=P)).then_inc(s_adj[g], 16)

            def diagonal(t):
                d = mask[:, t, t * P:(t + 1) * P]
                pool.wait_ge(s_adj[t // TC], 16)
                pool.affine_select(out=d, in_=d, compare_op=ALU.not_equal, fill=1.0, base=0,
                                   pattern=[[-1, P]], channel_multiplier=1).then_inc(s_diag, 1)

            def split(high, low, raw, loaded, loads, done, before):
                pool.wait_ge(loaded, loads)
                pool.sem_inc(s_pool_tick)
                pool.tensor_copy(high, raw).then_inc(done, 1)
                pool.wait_ge(done, before + 1)
                pool.tensor_tensor(low, raw, f32(high), ALU.subtract).then_inc(done, 1)

            def split_qk(h, off):
                split(wh[:, :, :, :], wl[:, :, :, :], raw_qk[:, :, :, :], s_rawqk, (h + 1) * 32 + off["qk"], s_wqk, 2 * h + off["head2"])

            def split_wo(h, off):
                split(woh[:, :], wol[:, :], raw_o[:, :], s_rawo, (h + 1) * 32 + off["wo"], s_wo, 2 * h + off["head2"])

            def split_v(h, half, off):
                ts = slice(half * (NT // 2), (half + 1) * (NT // 2))
                split(v[:, ts, 0:DK], v[:, ts, DK:2 * DK], raw_v[:, :, :], s_rawv, (2 * h + half - 1) * 16 + off["wo"],
                      s_v, 4 * h + 2 * half + off["v"])

            zero = dict.fromkeys(PER, 0)
            split_qk(0, zero)
            for t in range(TC):
                diagonal(t)
            split(wvh, wvl, wv_raw, s_rawwv, 16 * H, s_wv, 0)
            for t in range(TC, NT):
                diagonal(t)
            split_wo(0, zero)
            for half in range(2):
                ts = slice(half * (NT // 2), (half + 1) * (NT // 2))
                split(v[:, ts, 0:DK], v[:, ts, DK:2 * DK], v_stage[:, 0, ts, :], s_vcopied, (half + 1) * (NT // 2), s_v, 2 * half)

            def step(n, off):
                c, h = n % NC, n // NC
                if 2 <= n < LAST:
                    if c == 2 and h < H - 1:
                        pool.wait_ge(s_wqk_used, h + 1 + off["head"])
                        split_qk(h + 1, off)
                    if c == 1:
                        pool.wait_ge(s_pv, n - 1 + off["chunk"])
                        split_v(h, 1, off)
                if n >= 2:
                    m = n - 2
                    for half in range(2):
                        pool.wait_ge(s_y, m * TC + 2 * half + 2 + off["tile"])
                        if m > 0 or half > 0:
                            pool.wait_ge(s_add, m * 2 + half + off["y"])
                        xt = xacc[:, m % NC * TC + 2 * half:m % NC * TC + 2 * half + 2, :]
                        pool.tensor_tensor(xt, xt, y[:, :, :], ALU.add).then_inc(s_add, 1)
                if 2 <= n < LAST:
                    if c == 0:
                        pool.wait_ge(s_v_used, h + off["head"])
                        split_v(h, 0, off)
                    if c == 1:
                        pool.wait_ge(s_wo_used, h + off["head"])
                        split_wo(h, off)

            attention(pool, step, ("tile", "chunk", "y", "v", "head", "head2", "qk", "wo"))

        @block.tensor
        def _(pe):
            pe.wait_ge(s_ident, 2)
            for g in range(NT // TC):
                if g >= 2:
                    pe.wait_ge(s_lnl, g - 1)
                for t in range(TC):
                    pe.wait_ge(s_xn, g * TC + t + 1)
                    for j in range(J):
                        last = pe.transpose(slots[g % 2][:, j * CQ + t * P:j * CQ + (t + 1) * P],
                                            pr[:, g % 2 * TC + t, j * P:(j + 1) * P], ident[:, :])
                last.then_inc(s_lnt, 1)
            pe.wait_ge(s_lnl, NT // TC)

            def triple(o, lh, ll, rh, rl, first, last):
                pe.matmul(o, lh, rh, start=first, stop=False)
                pe.matmul(o, ll, rh, start=False, stop=False)
                return pe.matmul(o, lh, rl, start=False, stop=last)

            def slot(n, it, half, off):
                k = SLOT[n, it, half]
                if k >= 2:
                    pe.wait_ge(s_free[k % 2], k // 2 + off["buf"])
                return slots[k % 2]

            def times_v(m, kt, off):
                g = m * NT + kt
                if kt == 0 and m >= 1:
                    pe.wait_ge(s_ol, m + off["chunk"])
                if kt % (NT // 2) == 0 and m % NC == 0:
                    pe.wait_ge(s_v, 4 * (m // NC) + 2 + 2 * (kt // (NT // 2)) + off["v"])
                pe.wait_ge(s_pl, g + 1 + off["kt"])
                pe.matmul(po[:, :], v[:, kt, :], ph[:, kt % RING, :], start=(kt == 0), stop=False)
                last = pe.matmul(po[:, :], v[:, kt, :], pl[:, kt % RING, :], start=False, stop=(kt == NT - 1))
                if kt == NT - 1:
                    last.then_inc(s_pv, 1)
                elif kt == NT // 2 - 1 and m % NC == NC - 1:
                    last.then_inc(s_v_used, 1)

            def step(n, off):
                for it in plan(n):
                    kind = it[0]
                    if kind == "K":
                        a = it[1]
                        o = slot(n, it, 0, off)
                        if a == 0:
                            pe.wait_ge(s_wqk, 2 * ((n + 1) // NC + 1) + off["head2"])
                        for b in range(2):
                            for j in range(J):
                                cols = slice((2 * a + b) * CQ, (2 * a + b + 1) * CQ)
                                last = triple(o[:, b * CQ:(b + 1) * CQ], wh[:, j, :, :], wl[:, j, :, :],
                                              xhT[:, j, cols], xlT[:, j, cols], j == 0, j == J - 1)
                        last.then_inc(s_slot, 1)
                        if a == 1:
                            pe.wait_ge(s_slot, SLOT[n, it, 0] + 1 + off["slot"])
                            pe.sem_inc(s_wqk_used)
                    elif kind == "V":
                        t = it[1]
                        if t == 0:
                            pe.wait_ge(s_wv, 2)
                        if t >= WAYS:
                            pe.wait_ge(s_vcopied, t - WAYS + 1)
                        nodes = slice(t * P, (t + 1) * P)
                        for j in range(J):
                            cols = slice(j * H * DK, (j + 1) * H * DK)
                            last = triple(pts[t % WAYS][:, :], xhT[:, j, nodes], xlT[:, j, nodes],
                                          wvh[:, cols], wvl[:, cols], j == 0, j == J - 1)
                        last.then_inc(s_vall, 1)
                    elif kind == "S":
                        _, t, half = it
                        o = slot(n, it, 0, off)
                        if t == 0 and half == 0 and n % NC == 0:
                            for a in range(2):
                                k = SLOT[max(n - 1, 0), ("K", a), 0]
                                pe.wait_ge(s_free[k % 2], k // 2 + 1 + off["buf"])
                            pe.wait_ge(s_copied, 64 * (n // NC + 1) + off["copies"])
                        first = n % NC * CQ + t * P
                        qt = q[:, first:first + P]
                        for b in range(2):
                            cols = slice((2 * half + b) * CQ, (2 * half + b + 1) * CQ)
                            pe.matmul(o[:, b * CQ:(b + 1) * CQ], qt, kh[:, cols], start=True, stop=False)
                            last = pe.matmul(o[:, b * CQ:(b + 1) * CQ], qt, kl[:, cols], start=False, stop=True)
                        last.then_inc(s_slot, 1)
                    elif kind == "P":
                        m = n - 1
                        for kt in (2 * it[1], 2 * it[1] + 1):
                            g = m * NT + kt
                            if kt == 0:
                                if m == 0:
                                    pe.wait_ge(s_vcopied, NT)
                                pe.wait_ge(s_prob, 2 * TC * n + off["half_tile"])
                                if m >= 1:
                                    pe.wait_ge(s_pl, g + off["kt"])
                            elif kt >= WAYS:
                                pe.wait_ge(s_pl, g - WAYS + 1 + off["kt"])
                            for t in range(TC):
                                last = pe.transpose(pts[kt % WAYS][:, t * P:(t + 1) * P],
                                                    pr[:, m % 2 * TC + t, kt * P:(kt + 1) * P], ident[:, :])
                            last.then_inc(s_pt, 1)
                            if kt >= LAG:
                                times_v(m, kt - LAG, off)
                    elif kind == "E":
                        for kt in range(NT - LAG, NT):
                            times_v(n - 2, kt, off)
                    elif kind == "W":
                        m = n - 2
                        o = slot(n, it, 0, off)
                        pe.wait_ge(s_ol, m + 1 + off["chunk"])
                        if m % NC == 0:
                            pe.wait_ge(s_wo, 2 * (m // NC + 1) + off["head2"])
                        for t in range(TC):
                            cols = slice(t * P, (t + 1) * P)
                            last = triple(o[:, t * D:(t + 1) * D], oh[:, cols], ol[:, cols], woh[:, :], wol[:, :], True, True)
                        last.then_inc(s_slot, 1)
                        if m % NC == NC - 1:
                            pe.wait_ge(s_slot, SLOT[n, it, 0] + 1 + off["slot"])
                            pe.sem_inc(s_wo_used)

            attention(pe, step, ("slot", "buf", "kt", "half_tile", "chunk", "v", "head2", "copies"))

        @block.scalar
        def _(act):
            act.wait_ge(s_stat, 2 * NT + 1)
            act.activation(sd[:, :], mv[:, :, 1], ACT.Sqrt, bias=epsc[:, 0:1]).then_inc(s_sd, 1)
            for g in range(NT // TC):
                act.wait_ge(s_lnt, g + 1)
                act.activation(xhT[:, :, g * CQ:(g + 1) * CQ], slots[g % 2][:, :].rearrange("p (j n) -> p j n", j=J),
                               ACT.Copy).then_inc(s_lnh, 1)

            def step(n, off):
                for it in scalar_plan(n):
                    kind = it[0]
                    if kind == "K":
                        k, cols = SLOT[n, it, 0], slice(it[1] * SLOT_W, (it[1] + 1) * SLOT_W)
                        act.wait_ge(s_slot, k + 1 + off["slot"])
                        act.activation(kh[DK:P, cols], slots[k % 2][DK:P, :], ACT.Copy).then_inc(s_hi, 1)
                        act.activation(q[0:DK, cols], slots[k % 2][0:DK, :], ACT.Copy, scale=Q_SCALE).then_inc(s_hi, 1)
                    elif kind == "V":
                        t = it[1]
                        act.wait_ge(s_vall, t + 1)
                        act.activation(v_stage[:, :, t, :], pts[t % WAYS][:, :].rearrange("p (h k) -> p h k", k=DK),
                                       ACT.Copy).then_inc(s_vcopied, 1)
                    elif kind == "X":
                        _, t, half = it
                        i, cols = n % 2 * TC + t, slice(half * SLOT_W, (half + 1) * SLOT_W)
                        act.wait_ge(s_max, n * TC + t + 1 + off["tile"])
                        act.activation(pr[:, i, cols], pr[:, i, cols], ACT.Exp, bias=nbias[:, i:i + 1], scale=EXP_SCALE,
                                       accum_out=rsum[:, n % 2, half, t:t + 1]).then_inc(s_prob, 1)
                    elif kind == "P":
                        for kt in (2 * it[1], 2 * it[1] + 1):
                            act.wait_ge(s_pt, (n - 1) * NT + kt + 1 + off["kt"])
                            act.activation(ph[:, kt % RING, :], pts[kt % WAYS][:, :], ACT.Copy).then_inc(s_ph, 1)
                    elif kind == "E":
                        act.wait_ge(s_pv, n - 1 + off["chunk"])
                        act.activation(oh[:, :], po[:, :], ACT.Copy).then_inc(s_oh, 1)
                    elif kind == "W":
                        m, k, half = n - 2, SLOT[n, ("W",), 0], it[1]
                        act.wait_ge(s_slot, k + 1 + off["slot"])
                        act.wait_ge(s_rinv, m + 1 + off["chunk"])
                        if m == 0 and half == 0:
                            act.wait_ge(s_rows_zero, 16)
                        if m * 2 + half > 0:
                            act.wait_ge(s_add, m * 2 + half + off["y"])
                        for t in (2 * half, 2 * half + 1):
                            act.activation(y[:, t % 2, :], slots[k % 2][:, t * D:(t + 1) * D], ACT.Copy,
                                           scale=rinv[:, m % 2, t:t + 1]).then_inc(s_y, 1)
                        if half == 1:
                            act.wait_ge(s_y, (m + 1) * TC + off["tile"])
                            act.sem_inc(s_free[k % 2])

            attention(act, step, ("slot", "kt", "tile", "chunk", "y"))

        @block.vector
        def _(dve):
            dve.memset(epsc[:, :], LN_EPS).then_inc(s_stat, 1)
            for t in range(NT):
                if t % TC == 0:
                    dve.wait_ge(s_x[t // TC], 16)
                dve.bn_stats(stats[:, t, :], xacc[:, t, :]).then_inc(s_stat, 1)
            for t in range(NT):
                dve.wait_ge(s_stat, t + 2)
                dve.bn_aggr(mv[:, t, :], stats[:, t, :]).then_inc(s_stat, 1)
            dve.wait_ge(s_sd, 1)
            dve.reciprocal(rstd[:, :], sd[:, :]).then_inc(s_stat, 1)
            dve.wait_ge(s_stat, 2 * NT + 2)

            def split_rows(g):
                dve.wait_ge(s_lnh, g + 1)
                dve.tensor_tensor(xlT[:, :, g * CQ:(g + 1) * CQ], slots[g % 2][:, :].rearrange("p (j n) -> p j n", j=J),
                                  f32(xhT[:, :, g * CQ:(g + 1) * CQ]), ALU.subtract).then_inc(s_lnl, 1)

            for g in range(NT // TC):
                for t in range(TC):
                    tt = g * TC + t
                    if g >= 2:
                        dve.wait_ge(s_lnt, g - 1)
                    dve.tensor_scalar(pr[:, g % 2 * TC + t, 0:D], xacc[:, tt, :], mv[:, tt, 0:1], rstd[:, tt:tt + 1],
                                      ALU.subtract, ALU.mult).then_inc(s_xn, 1)
                if g >= 1:
                    split_rows(g - 1)
            split_rows(NT // TC - 1)

            unmasked = list(range(NT))

            def masks(count):
                for t in unmasked[:count]:
                    dve.wait_ge(s_diag, t + 1)
                    dve.tensor_scalar(mask[:, t, :], mask[:, t, :], -1.0, None, ALU.add).then_inc(s_mask, 1)
                del unmasked[:count]

            masks(1)

            def step(n, off):
                for it in plan(n):
                    kind = it[0]
                    if n == 0 and kind in ("K", "S"):
                        masks(2 if kind == "S" and it[1] > 0 else 1)
                    if kind == "K":
                        k, cols = SLOT[n, it, 0], slice(it[1] * SLOT_W, (it[1] + 1) * SLOT_W)
                        o, hi = slots[k % 2], 2 * HI[n, it, 0]
                        dve.wait_ge(s_hi, hi + 1 + off["two_hi"])
                        dve.tensor_tensor(kl[DK:P, cols], o[DK:P, :], f32(kh[DK:P, cols]), ALU.subtract).then_inc(s_kl, 1)
                        dve.wait_ge(s_kl, HI[n, it, 0] + 1 + off["hi"])
                        dve.wait_ge(s_hi, hi + 2 + off["two_hi"])
                        dve.scalar_tensor_tensor(q[DK:P, cols], o[0:DK, :], Q_SCALE, f32(q[0:DK, cols]),
                                                 ALU.mult, ALU.subtract).then_inc(s_free[k % 2], 1)
                    elif kind == "S":
                        _, t, half = it
                        i, qt, k = n % 2 * TC + t, n % NC * TC + t, SLOT[n, it, 0]
                        if n == 0:
                            dve.wait_ge(s_mask, t + 1)
                        if n == 1 and t == 0 and half == 0:
                            dve.wait_ge(s_mask, NT)
                            dve.wait_ge(s_vstored, 16 * (NT // TC))
                            dve.wait_ge(s_v, 4)
                        dve.wait_ge(s_slot, k + 1 + off["slot"])
                        dve.sem_inc(s_tick)
                        cols = slice(half * SLOT_W, (half + 1) * SLOT_W)
                        dve.tensor_tensor_reduce(pr[:, i, cols], slots[k % 2][:, :], mask[:, qt, cols], 1.0, -3.0e38,
                                                 ALU.add, ALU.max, mx[:, i, half:half + 1]).then_inc(s_free[k % 2], 1)
                        if half == 1:
                            for kk in (SLOT[n, ("S", t, 0), 0], k):
                                dve.wait_ge(s_free[kk % 2], kk // 2 + 1 + off["buf"])
                            dve.tensor_scalar(nbias[:, i:i + 1], mx[:, i, 0:1], mx[:, i, 1:2], -EXP_SCALE,
                                              ALU.max, ALU.mult).then_inc(s_max, 1)
                    elif kind == "P":
                        m = n - 1
                        for kt in (2 * it[1], 2 * it[1] + 1):
                            dve.wait_ge(s_ph, m * NT + kt + 1 + off["kt"])
                            dve.tensor_tensor(pl[:, kt % RING, :], pts[kt % WAYS][:, :], f32(ph[:, kt % RING, :]), ALU.subtract).then_inc(s_pl, 1)
                            if kt == 0:
                                dve.tensor_tensor(rinv[:, m % 2, :], rsum[:, m % 2, 0, :], rsum[:, m % 2, 1, :], ALU.add).then_inc(s_rsum, 1)
                            if kt == 1:
                                dve.wait_ge(s_rsum, m + 1 + off["chunk"])
                                dve.reciprocal(rinv[:, m % 2, :], rinv[:, m % 2, :]).then_inc(s_rinv, 1)
                    elif kind == "E":
                        dve.wait_ge(s_oh, n - 1 + off["chunk"])
                        dve.tensor_tensor(ol[:, :], po[:, :], f32(oh[:, :]), ALU.subtract).then_inc(s_ol, 1)

            attention(dve, step, ("slot", "buf", "kt", "chunk", "hi", "two_hi"))

            dve.wait_ge(s_add, 2 * (LAST - 1))
            done = 2 * NT + 2
            for t in range(NT - TC):
                dve.bn_stats(stats[:, t, :], xacc[:, t, :]).then_inc(s_stat, 1)
            for t in range(NT - TC):
                dve.wait_ge(s_stat, done + t + 1)
                dve.bn_aggr(mv[:, t, :], stats[:, t, :]).then_inc(s_stat, 1)


def routed_tiles(N, E):
    tiles = (2 * N + (P - 1) * E) // P
    return -(-tiles // 4) * 4


def expert_block(nc, sem, xacc, stats, mv, ident, xs, gate_w, gate_b, shared_w1, shared_b1, shared_w2, shared_b2, shared_act,
                 expert_w1, expert_b1, expert_w2, expert_b2, expert_act, out):
    D = gate_w.shape[0]
    E = gate_w.shape[1]
    HID = shared_w1.shape[1]
    I = HID // 2
    NT = xacc.shape[1]
    N = NT * P
    J = D // P
    KI = 96
    JI = I // KI
    TOPK = 2
    TILES = routed_tiles(N, E)
    ALL = NT + TILES
    UNROLL = 4
    PACK = 1 << (E - 1).bit_length()
    assert PACK ** UNROLL <= 1 << 24
    DEPTH = 4
    LOOP = NT + 2 * UNROLL
    assert ALL % UNROLL == 0 and NT % UNROLL == 0
    JT = N // P
    GATHER = 4
    COUNT_TURN = 1
    KNOWN = NT - 4
    NACT = 7

    with ExitStack() as ctx:
        def sb(name, shape, dt=F32):
            return ctx.enter_context(nc.sbuf_tensor(name, shape, dt))

        def psum(name, shape, dt=F32):
            return ctx.enter_context(nc.psum_tensor(name, shape, dt))

        ys = nc.dram_tensor("expert_results", [TILES * P, D], F32, kind="Internal").ap()

        w1 = sb("w1", [P, E + 1, J, HID])
        w2 = sb("w2", [KI, E + 1, JI, D])
        b1 = sb("b1", [P, E + 1, HID])
        b2 = sb("b2", [P, E + 1, D])
        gw = sb("gw", [P, J, E])
        gb = sb("gb", [P, E])
        araw = sb("araw", [P, E + 1, 5])
        acts = sb("acts", [P, E + 1, NACT])
        clamp = sb("clamp", [P, 4, E + 1, 2])
        ones = sb("ones", [P, P])
        before = sb("before", [P, P])
        iota_e = sb("iota_e", [P, E])
        iota_t = sb("iota_t", [P, TILES])
        iota_j = sb("iota_j", [P, JT])
        xn = sb("xn2", [P, NT, D])
        sd = sb("sd2", [P, NT])
        rstd = sb("rstd2", [P, NT])
        epsc = sb("epsc2", [P, 1])
        xT = sb("xT", [P, 2, J, P])
        logits = sb("logits", [P, NT, E])
        top = sb("top", [P, NT, 8])
        topi = sb("topi", [P, NT, 8], U32)
        topf = sb("topf", [P, TOPK, NT])
        diff = sb("diff", [P, NT])
        cw = sb("cw", [P, TOPK, NT])
        oh = sb("onehot", [P, TOPK, NT, E])
        oh12 = sb("oh12", [P, NT, E])
        big = sb("big", [P, E * TILES])
        ntile = sb("ntile", [P, 5, E])
        upto = sb("upto", [P, 2, NT, E])
        place = sb("place", [P, NT, E])
        slotf = sb("slotf", [P, TOPK, NT])
        slot = sb("slot", [P, TOPK, NT], U32)
        eidf = sb("eidf", [P, TILES])
        packf = sb("packf", [P, TILES // UNROLL])
        packed = sb("packed", [P, TILES // UNROLL], I32)
        xin = sb("xin", [P, UNROLL, D])
        hb = sb("hb", [P, 2, HID])
        gg = sb("gg", [P, 2, I])
        uu = sb("uu", [P, 2, I])
        sg = sb("sg", [P, 2, I])
        te = sb("te", [P, 2, I])
        teT = sb("teT", [KI, 2, JI, P])
        yo = sb("yo", [P, UNROLL, D])
        yg = sb("yg", [P, GATHER, TOPK, D])

        gate_xT = xin[:, :, :].rearrange("p (b h) (j n) -> p b (h j) n", b=2, n=P)

        ps_x = psum("ps_x", [P, 512])
        ps_te = psum("ps_te", [P, 512])
        ps_h = [psum(f"ps_h{i}", [P, 512]) for i in range(2)]
        ps_y = [psum(f"ps_y{i}", [P, 512]) for i in range(2)]
        ps_place = psum("ps_place", [P, 512])
        ps_count = psum("ps_count", [P, 512])

        s_w = sem("e_weights")
        s_ws = sem("e_shared_weights")
        s_gate = sem("e_gate_weights")
        s_act = sem("e_act_table")
        s_const = sem("e_constants")
        s_ln = sem("e_ln")
        s_lnsd = sem("e_lnsd")
        s_xn = sem("e_xn")
        s_gt = sem("e_gate_transposed")
        s_gx = sem("e_gate_copied")
        s_gl = sem("e_gate_logits")
        s_top = sem("e_top")
        s_cw = sem("e_top_weights")
        s_oh = sem("e_onehot")
        s_cnt = sem("e_counts")
        s_chain = sem("e_chain")
        s_place = sem("e_place")
        s_eid = sem("e_eid")
        s_clampt = sem("e_softplus")
        s_biased = sem("e_biased")
        s_scat = sem("e_scattered")
        s_xin = [sem(f"e_xin{b}") for b in range(UNROLL)]
        s_xt = sem("e_xt")
        s_xc = sem("e_xc")
        s_h = sem("e_h")
        s_hb = sem("e_hb")
        s_clip = sem("e_clip")
        s_gated = sem("e_gated")
        s_sig = sem("e_sig")
        s_te = sem("e_te")
        s_tt = sem("e_tt")
        s_tc = sem("e_tc")
        s_y = sem("e_y")
        s_yo = sem("e_yo")
        s_ys = [sem(f"e_ys{b}") for b in range(UNROLL)]
        s_yg = [sem(f"e_yg{b}") for b in range(GATHER)]
        s_sum = sem("e_sum")
        s_res = sem("e_res")
        s_out = sem("e_out")

        block = ctx.enter_context(nc.Block())

        def turns(eng, turn):
            def body(quad, count=UNROLL):
                experts = tile_experts(eng, quad - 1)
                for k in range(count):
                    turn(quad, k, experts)
                    if k == 0:
                        experts += tile_experts(eng, quad)

            for quad in range(LOOP // UNROLL):
                body(quad)
            with eng.Fori(LOOP // UNROLL, ALL // UNROLL) as quad:
                body(quad)
            body(ALL // UNROLL, DEPTH)

        def tile(eng, quad, k, back):
            if isinstance(quad, int):
                i = quad * UNROLL + k - back
                return i if 0 <= i < ALL else None
            return quad * UNROLL + (k - back)

        def is_shared(i):
            return isinstance(i, int) and i < NT

        def scalar_of(i, value, number):
            e = slice(E, E + 1) if is_shared(i) else bass.ds(value, 1)
            return acts[:, e, number]

        def tile_experts(eng, quad):
            if isinstance(quad, int) and not NT // UNROLL <= quad < ALL // UNROLL:
                return [None] * UNROLL
            word = eng.value_load(packed[0:1, bass.ds(quad - NT // UNROLL, 1)], min_val=0, max_val=PACK ** UNROLL - 1)
            return [eng.snap(word // PACK ** k % PACK) for k in range(UNROLL)]

        @block.sync
        def _(sp):
            sp.dma_start(gw[:, :, :], gate_w.rearrange("(j p) e -> p j e", p=P)).then_inc(s_gate, 16)
            sp.dma_start(gb[:, :], gate_b.rearrange("(a e) -> a e", a=1).broadcast_to([P, E])).then_inc(s_gate, 16)
            sp.dma_start(w1[:, E, :, :], shared_w1.rearrange("(j p) h -> p j h", p=P)).then_inc(s_ws, 16)
            sp.dma_start(b1[:, E, :], shared_b1.rearrange("(a h) -> a h", a=1).broadcast_to([P, HID])).then_inc(s_ws, 16)
            sp.dma_start(araw[:, 0:E, :], expert_act.rearrange("(a e) k -> a e k", a=1).broadcast_to([P, E, 5])).then_inc(s_act, 16)
            sp.dma_start(araw[:, E, :], shared_act.rearrange("(a k) -> a k", a=1).broadcast_to([P, 5])).then_inc(s_act, 16)
            sp.dma_start(b2[:, E, :], shared_b2.rearrange("(a h) -> a h", a=1).broadcast_to([P, D])).then_inc(s_ws, 16)
            sp.dma_start(w2[:, E, :, :], shared_w2.rearrange("(j p) d -> p j d", p=KI)).then_inc(s_ws, 16)
            for e in range(E):
                sp.dma_start(w1[:, e, :, :], expert_w1[e].rearrange("(j p) h -> p j h", p=P)).then_inc(s_w, 16)
                sp.dma_start(w2[:, e, :, :], expert_w2[e].rearrange("(j p) d -> p j d", p=KI)).then_inc(s_w, 16)
            sp.dma_start(b1[:, 0:E, :], expert_b1.rearrange("(a e) h -> a e h", a=1).broadcast_to([P, E, HID])).then_inc(s_w, 16)
            sp.dma_start(b2[:, 0:E, :], expert_b2.rearrange("(a e) h -> a e h", a=1).broadcast_to([P, E, D])).then_inc(s_w, 16)

            def load(quad, k):
                i = (quad - NT // UNROLL) * UNROLL + k
                sp.dma_start(xin[:, k, :], xs[bass.ds(i * P, P), :]).then_inc(s_xin[k], 16)

            sp.wait_ge(s_scat, 16 * TOPK * NT)
            sp.wait_ge(s_eid, 1)
            sp.wait_ge(s_w, 16 * (2 + 2 * E))
            for k in range(UNROLL):
                load(NT // UNROLL, k)
            with sp.Fori(NT // UNROLL + 1, ALL // UNROLL) as quad:
                for k in range(UNROLL):
                    sp.wait_ge(s_xt, quad * UNROLL + (k - UNROLL + 1))
                    load(quad, k)
            for t in range(NT):
                sp.wait_ge(s_res, t + 1)
                sp.dma_start(out[t * P:(t + 1) * P, :], xacc[:, t, :]).then_inc(s_out, 16)
            sp.wait_ge(s_out, 16 * NT)

        @block.gpsimd
        def _(pool):
            pool.memset(ones[:, :], 1.0).then_inc(s_const, 1)
            pool.memset(before[:, :], 1.0).then_inc(s_const, 1)
            pool.wait_ge(s_const, 2)
            pool.affine_select(out=before[:, :], in_=before[:, :], compare_op=ALU.is_gt, fill=0.0, base=0,
                               pattern=[[1, P]], channel_multiplier=-1).then_inc(s_const, 1)
            pool.iota(iota_e[:, :], [[1, E]], base=0, channel_multiplier=0, allow_small_or_imprecise_dtypes=True).then_inc(s_const, 1)
            pool.iota(iota_t[:, :], [[1, TILES]], base=0, channel_multiplier=0, allow_small_or_imprecise_dtypes=True).then_inc(s_const, 1)
            pool.iota(iota_j[:, :], [[P, JT]], base=0, channel_multiplier=0, allow_small_or_imprecise_dtypes=True).then_inc(s_const, 1)
            pool.wait_ge(s_ws, 64)
            pool.wait_ge(s_xn, NT)
            for t in range(NT):
                pool.tensor_tensor(xacc[:, t, :], xacc[:, t, :], b2[:, E, :], ALU.add).then_inc(s_biased, 1)
            pool.wait_ge(s_place, 1)
            for k in range(TOPK):
                for t in range(NT):
                    pool.indirect_dma_start(xs, bass.IndirectOffsetOnAxis(slot[:, k, t:t + 1], 0),
                                            xn[:, t, :], None).then_inc(s_scat, 16)
            with pool.Fori(NT // UNROLL, ALL // UNROLL) as quad:
                for k in range(UNROLL):
                    pool.wait_ge(s_yo, quad * UNROLL + (k + 1))
                    i = (quad - NT // UNROLL) * UNROLL + k
                    pool.dma_start(ys[bass.ds(i * P, P), :], yo[:, k, :]).then_inc(s_ys[k], 16)
            for b in range(UNROLL):
                pool.wait_ge(s_ys[b], 16 * (TILES // UNROLL))
            for t in range(NT):
                b = t % GATHER
                if t >= GATHER:
                    pool.wait_ge(s_res, t - GATHER + 1)
                for k in range(TOPK):
                    pool.indirect_dma_start(yg[:, b, k, :], None, ys,
                                            bass.IndirectOffsetOnAxis(slot[:, k, t:t + 1], 0)).then_inc(s_yg[b], 16)

        @block.tensor
        def _(pe):
            pe.wait_ge(s_gate, 32)
            ps_g = [ps_x, ps_te]

            def gate_logits(pair):
                pe.wait_ge(s_gx, pair + 1)
                for t in (2 * pair, 2 * pair + 1):
                    for j in range(J):
                        last = pe.matmul(ps_place[:, t * E:(t + 1) * E], gate_xT[:, pair % 2, (t % 2) * J + j, :], gw[:, j, :],
                                         start=(j == 0), stop=(j == J - 1))
                last.then_inc(s_gl, 1)

            for pair in range(NT // 2):
                if pair >= 2:
                    pe.wait_ge(s_gx, pair - 1)
                for t in (2 * pair, 2 * pair + 1):
                    pe.wait_ge(s_xn, t + 1)
                    for j in range(J):
                        at = (t % 2 * J + j) * P
                        last = pe.transpose(ps_g[pair % 2][:, at:at + P], xn[:, t, j * P:(j + 1) * P], ident[:, :])
                last.then_inc(s_gt, 1)
                if pair >= 1:
                    gate_logits(pair - 1)
            gate_logits(NT // 2 - 1)

            def count():
                pe.wait_ge(s_oh, 1)
                pe.wait_ge(s_const, 3)
                pe.matmul(ps_place[:, 0:NT * E], before[:, :], oh12[:, :, :], start=True, stop=True)
                pe.matmul(ps_count[:, 0:NT * E], ones[:, :], oh12[:, :, :], start=True, stop=True).then_inc(s_cnt, 1)

            def weights(i, value):
                return slice(E, E + 1) if is_shared(i) else bass.ds(value, 1)

            def turn(quad, k, experts):
                i = tile(pe, quad, k, 0)
                if i is not None:
                    if is_shared(i):
                        src = xn[:, i, :]
                        if i > 0:
                            pe.wait_ge(s_xc, i)
                    else:
                        src = xin[:, k, :]
                        pe.wait_ge(s_xin[k], (quad - NT // UNROLL + 1) * 16)
                        pe.wait_ge(s_xc, i)
                    for j in range(J):
                        last = pe.transpose(ps_x[:, j * P:(j + 1) * P], src[:, j * P:(j + 1) * P], ident[:, :])
                    last.then_inc(s_xt, 1)
                i = tile(pe, quad, k, 1)
                if i is not None:
                    b, e = (k - 1) % 2, weights(i, experts[k + 3])
                    if is_shared(i) and i == 0:
                        pe.wait_ge(s_ws, 64)
                    pe.wait_ge(s_xc, i + 1)
                    if not isinstance(i, int) or i >= 2:
                        pe.wait_ge(s_hb, i - 1)
                    for j in range(J):
                        last = pe.matmul(ps_h[b][:, 0:HID], xT[:, b, j, :], w1[:, e, j, :], start=(j == 0), stop=(j == J - 1))
                    last.then_inc(s_h, 1)
                i = tile(pe, quad, k, 3)
                if i is not None:
                    b = (k - 3) % 2
                    pe.wait_ge(s_te, i + 1)
                    if not isinstance(i, int) or i >= 1:
                        pe.wait_ge(s_tc, i)
                    for j in range(JI):
                        last = pe.transpose(ps_te[0:KI, j * P:(j + 1) * P], te[:, b, j * KI:(j + 1) * KI], ident[:, :])
                    last.then_inc(s_tt, 1)
                i = tile(pe, quad, k, 4)
                if i is not None:
                    b, e = k % 2, weights(i, experts[k])
                    pe.wait_ge(s_tc, i + 1)
                    if not isinstance(i, int) or i >= 2:
                        pe.wait_ge(s_yo, i - 1)
                    for j in range(JI):
                        last = pe.matmul(ps_y[b][:, 0:D], teT[:, b, j, :], w2[:, e, j, :], start=(j == 0), stop=(j == JI - 1))
                    last.then_inc(s_y, 1)
                if isinstance(quad, int) and quad * UNROLL + k == COUNT_TURN:
                    count()

            turns(pe, turn)

        @block.scalar
        def _(act):
            act.wait_ge(s_ln, 1)
            act.activation(sd[:, 0:KNOWN], mv[:, 0:KNOWN, 1], ACT.Sqrt, bias=epsc[:, 0:1]).then_inc(s_lnsd, 1)
            act.wait_ge(s_ln, 2 * (NT - KNOWN) + 1)
            act.activation(sd[:, KNOWN:NT], mv[:, KNOWN:NT, 1], ACT.Sqrt, bias=epsc[:, 0:1]).then_inc(s_lnsd, 1)
            for pair in range(NT // 2):
                act.wait_ge(s_gt, pair + 1)
                if pair >= 2:
                    act.wait_ge(s_gl, pair - 1)
                act.activation(gate_xT[:, pair % 2, :, :], [ps_x, ps_te][pair % 2][:, :], ACT.Copy).then_inc(s_gx, 1)
                if pair == KNOWN // 2 - 1:
                    act.wait_ge(s_clampt, 3)
                    act.activation(clamp[:, 2, :, :], clamp[:, 1, :, :], ACT.Exp, scale=-1.0).then_inc(s_clampt, 1)
                    act.wait_ge(s_clampt, 4)
                    act.activation(clamp[:, 3, :, :], clamp[:, 2, :, :], ACT.Ln, bias=1.0).then_inc(s_clampt, 1)

            def turn(quad, k, experts):
                i = tile(act, quad, k, 2)
                if i is not None:
                    act.wait_ge(s_clip, i * 2 + 1)
                    act.activation(sg[:, k % 2, :], gg[:, k % 2, :], ACT.Sigmoid,
                                   scale=scalar_of(i, experts[k + 2], 0)).then_inc(s_sig, 1)
                i = tile(act, quad, k, 0)
                if i is not None:
                    act.wait_ge(s_xt, i + 1)
                    act.activation(xT[:, k % 2, :, :], ps_x[:, 0:J * P], ACT.Copy).then_inc(s_xc, 1)
                i = tile(act, quad, k, 3)
                if i is not None:
                    act.wait_ge(s_tt, i + 1)
                    act.activation(teT[:, (k - 3) % 2, :, :], ps_te[0:KI, 0:JI * P], ACT.Copy).then_inc(s_tc, 1)
                if isinstance(quad, int) and quad * UNROLL + k == COUNT_TURN:
                    act.wait_ge(s_top, 1)
                    act.activation(cw[:, 0, :], diff[:, :], ACT.Sigmoid, scale=-1.0).then_inc(s_cw, 1)
                    act.activation(cw[:, 1, :], diff[:, :], ACT.Sigmoid).then_inc(s_cw, 1)

            turns(act, turn)

        @block.vector
        def _(dve):
            chain = [0]

            def link(ins):
                chain[0] += 1
                ins.then_inc(s_chain, 1)

            def linked():
                dve.wait_ge(s_chain, chain[0])

            dve.memset(epsc[:, :], LN_EPS).then_inc(s_ln, 1)
            for t in range(KNOWN, NT):
                dve.bn_stats(stats[:, t, :], xacc[:, t, :]).then_inc(s_ln, 1)
            for t in range(KNOWN, NT):
                dve.wait_ge(s_ln, t - KNOWN + 2)
                dve.bn_aggr(mv[:, t, :], stats[:, t, :]).then_inc(s_ln, 1)
            groups = (slice(0, KNOWN), slice(KNOWN, NT))
            for group, tiles in enumerate(groups):
                dve.wait_ge(s_lnsd, group + 1)
                link(dve.reciprocal(rstd[:, tiles], sd[:, tiles]))
                linked()
                for t in range(tiles.start, tiles.stop):
                    dve.tensor_scalar(xn[:, t, :], xacc[:, t, :], mv[:, t, 0:1], rstd[:, t:t + 1],
                                      ALU.subtract, ALU.mult).then_inc(s_xn, 1)
                if group == 0:
                    dve.wait_ge(s_act, 32)
                    raw = araw[:, :, 3:5]
                    dve.tensor_scalar(clamp[:, 0, :, :], raw, -1.0, None, ALU.mult).then_inc(s_clampt, 1)
                    dve.wait_ge(s_clampt, 1)
                    dve.tensor_tensor(clamp[:, 1, :, :], raw, clamp[:, 0, :, :], ALU.max).then_inc(s_clampt, 1)
                    dve.wait_ge(s_clampt, 2)
                    dve.tensor_scalar(clamp[:, 0, :, :], raw, 0.0, None, ALU.max).then_inc(s_clampt, 1)
            dve.wait_ge(s_clampt, 5)
            link(dve.tensor_tensor(acts[:, :, 3:7:2], clamp[:, 0, :, :], clamp[:, 3, :, :], ALU.add))
            linked()
            link(dve.tensor_scalar(acts[:, :, 4:7:2], acts[:, :, 3:7:2], -1.0, None, ALU.mult))
            link(dve.tensor_copy(acts[:, :, 0:3], araw[:, :, 0:3]))

            def routing():
                dve.wait_ge(s_gl, NT // 2)
                link(dve.tensor_tensor(logits[:, :, :], ps_place[:, 0:NT * E].rearrange("p (t e) -> p t e", e=E),
                                       gb[:, :].rearrange("p (a e) -> p a e", a=1).broadcast_to([P, NT, E]), ALU.add))
                linked()
                for t in range(NT):
                    link(dve.max(top[:, t, :], logits[:, t, :]))
                yield
                linked()
                dve.tensor_tensor(diff[:, :], top[:, :, 1], top[:, :, 0], ALU.subtract).then_inc(s_top, 1)
                for t in range(NT):
                    link(dve.max_index(topi[:, t, :], top[:, t, :], logits[:, t, :]))
                yield
                linked()
                link(dve.tensor_copy(topf[:, :, :].rearrange("p k t -> p t k"), topi[:, :, 0:TOPK]))
                dve.wait_ge(s_const, 6)
                linked()
                for k in range(TOPK):
                    link(dve.tensor_tensor(oh[:, k, :, :], topf[:, k, :].rearrange("p (t a) -> p t a", a=1).broadcast_to([P, NT, E]),
                                           iota_e[:, :].rearrange("p (a e) -> p a e", a=1).broadcast_to([P, NT, E]), ALU.is_equal))
                linked()
                dve.tensor_tensor(oh12[:, :, :], oh[:, 0, :, :], oh[:, 1, :, :], ALU.add).then_inc(s_oh, 1)
                yield
                dve.wait_ge(s_cnt, 1)
                counts = ps_count[:, 0:NT * E].rearrange("p (t e) -> p t e", e=E)
                link(dve.tensor_copy(upto[:, 0, :, :], counts))
                linked()
                a, step = 0, 1
                while step < NT:
                    link(dve.tensor_copy(upto[:, 1 - a, 0:step, :], upto[:, a, 0:step, :]))
                    link(dve.tensor_tensor(upto[:, 1 - a, step:NT, :], upto[:, a, step:NT, :], upto[:, a, 0:NT - step, :], ALU.add))
                    linked()
                    a, step = 1 - a, 2 * step
                cnt = upto[:, a, NT - 1, :]
                link(dve.tensor_tensor(place[:, :, :], upto[:, a, :, :], counts, ALU.subtract))
                linked()
                link(dve.tensor_tensor(place[:, :, :], ps_place[:, 0:NT * E].rearrange("p (t e) -> p t e", e=E), place[:, :, :], ALU.add))
                cmp = big[:, 0:E * JT].rearrange("p (e j) -> p e j", j=JT)
                link(dve.tensor_tensor(cmp, cnt.rearrange("p (e a) -> p e a", a=1).broadcast_to([P, E, JT]),
                                       iota_j[:, :].rearrange("p (a j) -> p a j", a=1).broadcast_to([P, E, JT]), ALU.is_gt))
                linked()
                link(dve.tensor_reduce(ntile[:, 0, :], cmp, AX_X, ALU.add))
                linked()
                link(dve.tensor_copy(ntile[:, 1, :], ntile[:, 0, :]))
                linked()
                cur, step = 1, 1
                while step < E:
                    link(dve.tensor_copy(ntile[:, 3 - cur, 0:step], ntile[:, cur, 0:step]))
                    link(dve.tensor_tensor(ntile[:, 3 - cur, step:E], ntile[:, cur, step:E], ntile[:, cur, 0:E - step], ALU.add))
                    linked()
                    cur, step = 3 - cur, 2 * step
                link(dve.tensor_tensor(ntile[:, 3, :], ntile[:, cur, :], ntile[:, 0, :], ALU.subtract))
                linked()
                link(dve.tensor_scalar(ntile[:, 4, :], ntile[:, 3, :], float(P), None, ALU.mult))
                linked()
                link(dve.tensor_tensor(place[:, :, :], place[:, :, :],
                                       ntile[:, 4, :].rearrange("p (a e) -> p a e", a=1).broadcast_to([P, NT, E]), ALU.add))
                linked()
                for k in range(TOPK):
                    link(dve.tensor_tensor(oh[:, k, :, :], oh[:, k, :, :], place[:, :, :], ALU.mult))
                linked()
                for k in range(TOPK):
                    link(dve.tensor_reduce(slotf[:, k, :], oh[:, k, :, :], AX_X, ALU.add))
                linked()
                dve.tensor_copy(slot[:, :, :], slotf[:, :, :]).then_inc(s_place, 1)
                yield
                ends = big[:, :].rearrange("p (t e) -> p t e", e=E)
                link(dve.tensor_tensor(ends, ntile[:, cur, :].rearrange("p (a e) -> p a e", a=1).broadcast_to([P, TILES, E]),
                                       iota_t[:, :].rearrange("p (t a) -> p t a", a=1).broadcast_to([P, TILES, E]), ALU.is_le))
                linked()
                link(dve.tensor_reduce(eidf[:, :], ends, AX_X, ALU.add))
                linked()
                link(dve.tensor_scalar(eidf[:, :], eidf[:, :], float(E - 1), None, ALU.min))
                linked()
                digits = eidf[:, :].rearrange("p (q k) -> p q k", k=UNROLL)
                link(dve.tensor_copy(packf[:, :], digits[:, :, UNROLL - 1]))
                linked()
                for k in reversed(range(UNROLL - 1)):
                    link(dve.scalar_tensor_tensor(packf[:, :], packf[:, :], float(PACK), digits[:, :, k], ALU.mult, ALU.add))
                    linked()
                dve.tensor_copy(packed[:, :], packf[:, :]).then_inc(s_eid, 1)
                yield

            parts = routing()
            for _ in range(3):
                next(parts)

            def weights(i, value):
                return slice(E, E + 1) if is_shared(i) else bass.ds(value, 1)

            def turn(quad, k, experts):
                i, j, l = (tile(dve, quad, k, back) for back in (1, 2, 4))
                if j is not None:
                    b, scale = k % 2, scalar_of(j, experts[k + 2], 1)
                    dve.wait_ge(s_sig, j + 1)
                    dve.scalar_tensor_tensor(sg[:, b, :], gg[:, b, :], scale, sg[:, b, :], ALU.mult, ALU.mult).then_inc(s_gated, 1)
                if i is not None:
                    e = weights(i, experts[k + 3])
                    dve.wait_ge(s_h, i + 1)
                    if not isinstance(i, int) or i >= 2:
                        dve.wait_ge(s_te, i - 1)
                    dve.tensor_tensor(hb[:, (k - 1) % 2, :], ps_h[(k - 1) % 2][:, 0:HID], b1[:, e, :].rearrange("p a h -> p (a h)"),
                                      ALU.add).then_inc(s_hb, 1)
                if j is not None:
                    b, shift = k % 2, scalar_of(j, experts[k + 2], 2)
                    dve.wait_ge(s_gated, j + 1)
                    dve.scalar_tensor_tensor(te[:, b, :], uu[:, b, :], shift, sg[:, b, :], ALU.add, ALU.mult).then_inc(s_te, 1)
                if i is not None:
                    b = (k - 1) % 2
                    high, low, high_up, low_up = (scalar_of(i, experts[k + 3], n) for n in (3, 4, 5, 6))
                    dve.wait_ge(s_hb, i + 1)
                    dve.tensor_scalar(gg[:, b, :], hb[:, b, 0:HID:2], low, high, ALU.max, ALU.min).then_inc(s_clip, 1)
                    dve.tensor_scalar(uu[:, b, :], hb[:, b, 1:HID:2], low_up, high_up, ALU.max, ALU.min).then_inc(s_clip, 1)
                if l is not None:
                    y = ps_y[k % 2][:, 0:D]
                    dve.wait_ge(s_y, l + 1)
                    if is_shared(l):
                        dve.wait_ge(s_biased, l + 1)
                        dve.tensor_tensor(xacc[:, l, :], y, xacc[:, l, :], ALU.add).then_inc(s_yo, 1)
                    else:
                        e = weights(l, experts[k])
                        if not isinstance(l, int) or l >= NT + UNROLL:
                            dve.wait_ge(s_ys[k], (quad - NT // UNROLL - 1) * 16)
                        dve.tensor_tensor(yo[:, k, :], y, b2[:, e, :].rearrange("p a h -> p (a h)"), ALU.add).then_inc(s_yo, 1)
                if isinstance(quad, int) and quad * UNROLL + k > COUNT_TURN:
                    next(parts, None)

            turns(dve, turn)
            for t in range(NT):
                b = t % GATHER
                dve.wait_ge(s_yg[b], 16 * TOPK * (t // GATHER + 1))
                if t == 0:
                    dve.wait_ge(s_cw, 2)
                dve.scalar_tensor_tensor(xacc[:, t, :], yg[:, b, 0, :], cw[:, 0, t:t + 1], xacc[:, t, :], ALU.mult, ALU.add).then_inc(s_sum, 1)
                dve.wait_ge(s_sum, t + 1)
                dve.scalar_tensor_tensor(xacc[:, t, :], yg[:, b, 1, :], cw[:, 1, t:t + 1], xacc[:, t, :], ALU.mult, ALU.add).then_inc(s_res, 1)


def graph_attention_and_experts(nc, x, adj, Wks, Wqs, Wvs, Wo, gate_w, gate_b, shared_w1, shared_b1, shared_w2,
                                shared_b2, shared_act, expert_w1, expert_b1, expert_w2, expert_b2, expert_act, out):
    N, D = x.shape
    with ExitStack() as ctx:
        def sem(name):
            return ctx.enter_context(nc.semaphore(name))

        xacc = ctx.enter_context(nc.sbuf_tensor("xacc", [P, N // P, D], F32))
        stats = ctx.enter_context(nc.sbuf_tensor("stats", [P, N // P, 6], F32))
        mv = ctx.enter_context(nc.sbuf_tensor("mv", [P, N // P, 2], F32))
        ident = ctx.enter_context(nc.sbuf_tensor("ident", [P, P], F32))
        rows = nc.dram_tensor("expert_rows", [routed_tiles(N, gate_w.shape[1]) * P, D], F32, kind="Internal").ap()
        attention_block(nc, sem, xacc, stats, mv, ident, x, adj, Wks, Wqs, Wvs, Wo, rows)
        expert_block(nc, sem, xacc, stats, mv, ident, rows, gate_w, gate_b, shared_w1, shared_b1, shared_w2, shared_b2, shared_act,
                     expert_w1, expert_b1, expert_w2, expert_b2, expert_act, out)


_INS = ["x", "adj", "L0_gnn_Wks", "L0_gnn_Wqs", "L0_gnn_Wvs", "L0_gnn_Wo", "L0_ffn_gate_w", "L0_ffn_gate_b",
        "L0_ffn_shared_w1", "L0_ffn_shared_b1", "L0_ffn_shared_w2", "L0_ffn_shared_b2", "L0_ffn_shared_act",
        "L0_ffn_expert_w1", "L0_ffn_expert_b1", "L0_ffn_expert_w2", "L0_ffn_expert_b2", "L0_ffn_expert_act"]
_OUTS = [((2048, 256), "float32")]


def kernel(**inputs):
    import numpy as _np
    import concourse.bacc as _bacc
    from concourse import mybir as _mybir
    from concourse.bass_utils import run_bass_kernel_spmd as _run

    nc = _bacc.Bacc("TRN2", target_bir_lowering=False, num_devices=1)
    arrays, args = {}, []
    for name in _INS:
        a = _np.ascontiguousarray(inputs[name])
        arrays[f"in_{name}_dram"] = a
        args.append(nc.dram_tensor(f"in_{name}_dram", a.shape, _mybir.dt.from_np(a.dtype), kind="ExternalInput").ap())
    for i, (shape, dtype) in enumerate(_OUTS):
        dt = _mybir.dt.from_np(_np.dtype(dtype))
        args.append(nc.dram_tensor(f"out_{i}_dram", shape, dt, kind="ExternalOutput").ap())
    graph_attention_and_experts(nc, *args)
    r = _run(nc, [arrays], core_ids=[0])
    got = tuple(r.results[0][f"out_{i}_dram"] for i in range(len(_OUTS)))
    return got[0]
```
